# Optimizing a Trainium2 kernel written in Bass

```python
import numpy as np
import jax
import jax.numpy as jnp

def _softmax(x, axis=-1):
    return jax.nn.softmax(x, axis=axis)

def _gelu(x):
    return jax.nn.gelu(x, approximate=True)

def _silu(x):
    return jax.nn.silu(x)

def _sigmoid(x):
    return jax.nn.sigmoid(x)

def _layernorm(x, axis=-1, eps=1e-05):
    m = jnp.mean(x, axis=axis, keepdims=True)
    v = jnp.var(x, axis=axis, keepdims=True)
    return (x - m) / jnp.sqrt(v + eps)

def _scatter_add(tgt, idx, src, axis=0):
    return tgt.at[idx].add(src)

def _segment_sum(src, seg, n):
    return jax.ops.segment_sum(src, seg, n)
kernel_name = 'mk_vit_tower_d1_tok_img256_r4_9300f0'

def setup_inputs(seed: int=0):
    np.random.seed(seed)
    _w = jnp.asarray

    def _rec_inputs():
        import jax
        import jax.numpy as jnp
        _rk = jax.random.key(seed)
        x = 7.22013e-05 + 1.00017 * jax.random.normal(jax.random.fold_in(_rk, 1), (4, 1, 1024, 64), jnp.float32)
        return x
    x = _rec_inputs()

    def _L0_tok_setup():
        import jax, jax.numpy as jnp
        import numpy as np
        T, D_IN, D_INT, D_OUT, B = (1024, 64, 64, 64, 8)
        key = jax.random.key(seed)
        ks = jax.random.split(key, 12)
        s_in = 1.0 / np.sqrt(D_IN)
        s_int = 1.0 / np.sqrt(D_INT)
        return {'x_batched': jax.random.normal(ks[0], (B, 1, T, D_IN), dtype=jnp.float32), 'd_gamma_batched': jax.random.uniform(ks[1], (T, T), dtype=jnp.float32), 'Wq': jax.random.uniform(ks[2], (D_IN, D_INT), jnp.float32, -s_in, s_in), 'bq': jax.random.uniform(ks[3], (D_INT,), jnp.float32, -s_in, s_in), 'Wk': jax.random.uniform(ks[4], (D_IN, D_INT), jnp.float32, -s_in, s_in), 'bk': jax.random.uniform(ks[5], (D_INT,), jnp.float32, -s_in, s_in), 'Wv': jax.random.uniform(ks[6], (D_IN, D_INT), jnp.float32, -s_in, s_in), 'bv': jax.random.uniform(ks[7], (D_INT,), jnp.float32, -s_in, s_in), 'Wo': jax.random.uniform(ks[8], (D_INT, D_OUT), jnp.float32, -s_int, s_int), 'bo': jax.random.uniform(ks[9], (D_OUT,), jnp.float32, -s_int, s_int), 'prelu_a': jnp.float32(0.25)}
    _L0_tok_all = _L0_tok_setup()
    _L0_tok_in = {k: v for k, v in _L0_tok_all.items() if k in ('d_gamma_batched', 'Wq', 'bq', 'Wk', 'bk', 'Wv', 'bv', 'Wo', 'bo', 'prelu_a')}
    del _L0_tok_all

    def _L0_attn_setup():
        import jax, jax.numpy as jnp
        import numpy as np
        from jax import lax

        def _scan_combine(c1, c2):
            a1, b1 = c1
            a2, b2 = c2
            return (a1 * a2, a2 * b1 + b2)
        key = jax.random.key(seed)
        ks = jax.random.split(key, 6)
        B, L, Cin, N, Cout = (4, 1024, 64, 128, 64)
        s = 0.02
        return {'x': jax.random.normal(ks[0], (B, L, Cin), dtype=jnp.float32), 'Wx': jax.random.normal(ks[1], (Cin, N), dtype=jnp.float32) * s, 'bx': jnp.zeros((N,), dtype=jnp.float32), 'Wbc': jax.random.normal(ks[2], (Cin, 2 * N), dtype=jnp.float32) * s, 'bbc': jnp.zeros((2 * N,), dtype=jnp.float32), 'Wd': jax.random.normal(ks[3], (Cin, N), dtype=jnp.float32) * s, 'bd': jnp.zeros((N,), dtype=jnp.float32), 'Wy': jax.random.normal(ks[4], (N, Cout), dtype=jnp.float32) * s, 'by': jnp.zeros((Cout,), dtype=jnp.float32)}
    _L0_attn_all = _L0_attn_setup()
    _L0_attn_in = {k: v for k, v in _L0_attn_all.items() if k in ('Wx', 'bx', 'Wbc', 'bbc', 'Wd', 'bd', 'Wy', 'by')}
    del _L0_attn_all

    def _L0_ffn_setup():
        import jax, jax.numpy as jnp
        import numpy as np
        D_MODEL = 64
        N_EXPERTS = 16
        HIDDEN = 128
        SCALE = 0.02
        key = jax.random.key(seed)
        ks = jax.random.split(key, 5)
        x = jax.random.normal(ks[0], (4, 2048, D_MODEL), dtype=jnp.float32)
        gate_w = jax.random.normal(ks[1], (D_MODEL, N_EXPERTS), dtype=jnp.float32) * SCALE
        gate_b = jnp.zeros((N_EXPERTS,), dtype=jnp.float32)
        w1 = jax.random.normal(ks[2], (N_EXPERTS, D_MODEL, HIDDEN), dtype=jnp.float32) * SCALE
        w2 = jax.random.normal(ks[3], (N_EXPERTS, D_MODEL, HIDDEN), dtype=jnp.float32) * SCALE
        w3 = jax.random.normal(ks[4], (N_EXPERTS, HIDDEN, D_MODEL), dtype=jnp.float32) * SCALE
        return {'x': x, 'gate_w': gate_w, 'gate_b': gate_b, 'w1': w1, 'w2': w2, 'w3': w3}
    _L0_ffn_all = _L0_ffn_setup()
    _L0_ffn_in = {k: v for k, v in _L0_ffn_all.items() if k in ('gate_w', 'gate_b', 'w1', 'w2', 'w3')}
    del _L0_ffn_all
    return {'x': x, 'L0_tok_d_gamma_batched': _L0_tok_in['d_gamma_batched'], 'L0_tok_Wq': _L0_tok_in['Wq'], 'L0_tok_bq': _L0_tok_in['bq'], 'L0_tok_Wk': _L0_tok_in['Wk'], 'L0_tok_bk': _L0_tok_in['bk'], 'L0_tok_Wv': _L0_tok_in['Wv'], 'L0_tok_bv': _L0_tok_in['bv'], 'L0_tok_Wo': _L0_tok_in['Wo'], 'L0_tok_bo': _L0_tok_in['bo'], 'L0_tok_prelu_a': _L0_tok_in['prelu_a'], 'L0_attn_Wx': _L0_attn_in['Wx'], 'L0_attn_bx': _L0_attn_in['bx'], 'L0_attn_Wbc': _L0_attn_in['Wbc'], 'L0_attn_bbc': _L0_attn_in['bbc'], 'L0_attn_Wd': _L0_attn_in['Wd'], 'L0_attn_bd': _L0_attn_in['bd'], 'L0_attn_Wy': _L0_attn_in['Wy'], 'L0_attn_by': _L0_attn_in['by'], 'L0_ffn_gate_w': _L0_ffn_in['gate_w'], 'L0_ffn_gate_b': _L0_ffn_in['gate_b'], 'L0_ffn_w1': _L0_ffn_in['w1'], 'L0_ffn_w2': _L0_ffn_in['w2'], 'L0_ffn_w3': _L0_ffn_in['w3']}

def reference(x, L0_tok_d_gamma_batched, L0_tok_Wq, L0_tok_bq, L0_tok_Wk, L0_tok_bk, L0_tok_Wv, L0_tok_bv, L0_tok_Wo, L0_tok_bo, L0_tok_prelu_a, L0_attn_Wx, L0_attn_bx, L0_attn_Wbc, L0_attn_bbc, L0_attn_Wd, L0_attn_bd, L0_attn_Wy, L0_attn_by, L0_ffn_gate_w, L0_ffn_gate_b, L0_ffn_w1, L0_ffn_w2, L0_ffn_w3):
    import jax
    import jax.numpy as jnp

    def _L0_tok_ref(x_batched, d_gamma_batched, Wq, bq, Wk, bk, Wv, bv, Wo, bo, prelu_a):
        import jax, jax.numpy as jnp
        import numpy as np
        T, D_IN, D_INT, D_OUT, B = (1024, 64, 64, 64, 8)
        x = x_batched.reshape(x_batched.shape[0], T, D_IN)
        q = x @ Wq + bq
        k = x @ Wk + bk
        v = x @ Wv + bv
        scores = jnp.einsum('btd,bsd->bts', q, k)
        retained = jnp.einsum('bts,bsd->btd', d_gamma_batched * scores, v)
        y = retained @ Wo + bo
        out = jnp.where(y >= 0, y, prelu_a * y)
        return out

    def _L0_attn_ref(x, Wx, bx, Wbc, bbc, Wd, bd, Wy, by):
        import jax, jax.numpy as jnp
        import numpy as np
        from jax import lax

        def _scan_combine(c1, c2):
            a1, b1 = c1
            a2, b2 = c2
            return (a1 * a2, a2 * b1 + b2)
        x_proj = x @ Wx + bx
        BC = x @ Wbc + bbc
        delta = x @ Wd + bd
        Bm, C = jnp.split(BC, 2, axis=-1)
        A_bar = jnp.exp(-jax.nn.softplus(delta))
        B_bar = (1.0 - A_bar) * Bm
        u = B_bar * x_proj
        _, h = lax.associative_scan(_scan_combine, (A_bar, u), axis=1)
        y = C * h
        return y @ Wy + by

    def _L0_ffn_ref(x, gate_w, gate_b, w1, w2, w3):
        import jax, jax.numpy as jnp
        import numpy as np
        D_MODEL = 64
        N_EXPERTS = 16
        HIDDEN = 128
        SCALE = 0.02
        n_experts = w1.shape[0]
        logits = jnp.einsum('bsd,de->bse', x, gate_w) + gate_b
        probs = jax.nn.softmax(logits, axis=-1)
        top_probs, top_idx = jax.lax.top_k(probs, 2)
        top_probs = top_probs / jnp.sum(top_probs, axis=-1, keepdims=True)
        dispatch = jnp.sum(jax.nn.one_hot(top_idx, n_experts, dtype=x.dtype) * top_probs[..., None], axis=-2)
        h1 = jnp.einsum('bsd,edh->bseh', x, w1)
        h2 = jnp.einsum('bsd,edh->bseh', x, w2)
        hidden = jax.nn.silu(h1) * h2
        expert_out = jnp.einsum('bseh,eho->bseo', hidden, w3)
        return jnp.einsum('bseo,bse->bso', expert_out, dispatch)
    h = _L0_tok_ref(x, L0_tok_d_gamma_batched, L0_tok_Wq, L0_tok_bq, L0_tok_Wk, L0_tok_bk, L0_tok_Wv, L0_tok_bv, L0_tok_Wo, L0_tok_bo, L0_tok_prelu_a)
    h = h + _L0_attn_ref(_layernorm(h, axis=-1), L0_attn_Wx, L0_attn_bx, L0_attn_Wbc, L0_attn_bbc, L0_attn_Wd, L0_attn_bd, L0_attn_Wy, L0_attn_by)
    h = h + _L0_ffn_ref(_layernorm(h, axis=-1), L0_ffn_gate_w, L0_ffn_gate_b, L0_ffn_w1, L0_ffn_w2, L0_ffn_w3)
    return h

_drawn_inputs = setup_inputs


def setup_inputs(seed=0):
    import zlib

    import numpy as np

    out = dict(_drawn_inputs(seed))
    spreads = {'L0_attn_bx': (0.0, 0.8),
     'L0_attn_bbc': (0.0, 0.8),
     'L0_attn_bd': (0.0, 2.0),
     'L0_attn_by': (0.0, 2.0),
     'L0_ffn_gate_b': (0.0, 2.0)}
    factors = {'L0_tok_bo': 42.662,
     'L0_attn_Wx': 8.0,
     'L0_attn_Wbc': 8.0,
     'L0_attn_Wd': 8.0,
     'L0_attn_Wy': 8.0,
     'L0_ffn_gate_w': 8.0,
     'L0_ffn_w1': 8.0,
     'L0_ffn_w2': 8.0,
     'L0_ffn_w3': 8.0}
    for name, (base, spread) in spreads.items():
        noise = np.random.default_rng([zlib.crc32(name.encode()), seed]).standard_normal(out[name].shape)
        drawn = base * np.exp(spread * noise) if base else spread * noise
        out[name] = jnp.asarray(drawn.astype(out[name].dtype))
    for name, factor in factors.items():
        out[name] = (out[name] * factor).astype(out[name].dtype)
    return out
```

```python
from contextlib import ExitStack

import concourse.bass as bass
from concourse import mybir

F32 = mybir.dt.float32
F32R = mybir.dt.float32r
BF16 = mybir.dt.bfloat16
I32 = mybir.dt.int32
ALU = mybir.AluOpType
ACT = mybir.ActivationFunctionType
AX_X = mybir.AxisListType.X
PE_ENGINE = mybir.EngineType.PE

P = 128
NB, T, D = 4, 1024, 64
CH = 128
NE, HID = 16, 128
HALVES, UNITS = 2, 4
BH = NB // HALVES
CW = T // 2
JT = T // P
UT = BH * CW // P
HT = 2 * UT
STEPS = JT
BLOCKS = BH * T * 2 // P + NE
GB = 4
GROUPS = BLOCKS // GB
EPS = 1e-5
ZEROINGS = 4
LAST_TILES = 4
COMBINES = HT // LAST_TILES

Q0, K0, V0, X0, B0, C0, D0, G0, WCOLS = 0, 128, 256, 320, 448, 576, 704, 832, 848
BQ, BK, BX, BB, BC, BD, PRELU, NVEC = 0, 1, 2, 3, 4, 5, 6, 7
RV, RO, RY, RG, NROW = 0, 64, 128, 192, 208


def build_layer(nc, xT, dgT, wproj, vecs, rows, wo, wy, w12, w3, out):
    with ExitStack() as ctx:
        def sb(name, shape, dt=F32):
            return ctx.enter_context(nc.sbuf_tensor(name, shape, dt))

        def sem(name):
            return ctx.enter_context(nc.semaphore(name))

        slots_dram = [nc.dram_tensor(f"slots{h}", [BLOCKS * P, 2 * D], F32).ap() for h in range(HALVES)]
        results_dram = [nc.dram_tensor(f"results{h}", [BLOCKS * P, D], F32).ap() for h in range(HALVES)]

        x_raw = sb("x_raw", [P, NB * T])
        x_parts = sb("x_parts", [P, BH * T], F32R)
        qk = sb("qk", [P, HALVES, 3, BH * T], F32R)
        dg = sb("dg", [P, 2, JT, CW])
        v = sb("v", [P, HALVES, BH, JT, D])
        mixed = sb("mixed", [P, 2, BH, CW])
        ret = sb("ret", [P, CW])
        h = sb("h", [P, HALVES, HT, D])
        centered = sb("centered", [P, 2, UT, D])
        squares = sb("squares", [P, 2, UT, D])
        normed = squares
        prelu_neg = squares[:, 0]
        stats = sb("stats", [P, 2, 5, UT])
        ssm_rows = sb("ssm_rows", [P, UT, 2 * D])
        ffn_rows = sb("ffn_rows", [P, HALVES, HT, 2 * D])
        ssm_in = sb("ssm_in", [P, BH, CW], F32R)
        gate_in = sb("gate_in", [P, BH, CW], F32R)
        keep = sb("keep", [P, 2, CW])
        take = sb("take", [P, 2, CW])
        xb = sb("xb", [P, 2, CW])
        cb = sb("cb", [P, 2, CW])
        drive = take
        state = sb("state", [P, BH, 2, CW])
        read = cb
        w_raw = mixed[:, :, :, :].rearrange("p a b n -> p (a b n)")[:, 0:WCOLS]
        w_hi = sb("w_hi", [P, WCOLS], F32R)
        w_lo = sb("w_lo", [P, WCOLS], F32R)
        vec = sb("vec", [P, NVEC])
        neg_bd = sb("neg_bd", [P, 1])
        eps = sb("eps", [P, 1])
        row = sb("row", [P, NROW])
        wo_sb = sb("wo_sb", [P, D])
        wy_sb = sb("wy_sb", [P, D])
        ident = sb("ident", [P, P])
        before = sb("before", [P, P], BF16)
        ones = sb("ones", [P, P], BF16)
        rank_of = sb("rank_of", [P, NE])
        not_first = sb("not_first", [P, NE, HT])
        ones16 = sb("ones16", [P, NE])
        block_no = sb("block_no", [1, BLOCKS])
        iota_i = sb("iota_i", [P, BLOCKS], I32)
        zeros = sb("zeros", [P, 256])
        logits = sb("logits", [P, HT, NE])
        best = sb("best", [P, HALVES, 2, HT])
        top = sb("top", [P, 2, HT, NE])
        spare = [buf[:, 1].rearrange("p i d -> p (i d)") for buf in (centered, squares)]
        r_a, slot = (spare[1][:, k * HT * NE:(k + 1) * HT * NE].rearrange("p (i e) -> p i e", e=NE) for k in range(2))
        counts, counts_to = (spare[0][:, k * HT * NE:(k + 1) * HT * NE].rearrange("p (e i) -> p e i", i=HT)
                             for k in range(2))
        r_b = sb("r_b", [P, HT])
        chosen = sb("chosen", [P, HT, NE], BF16)
        n_int = sb("n_int", [P, NE], I32)
        n_blocks = sb("n_blocks", [P, NE])
        blocks_to = sb("blocks_to", [P, NE])
        first_slot = sb("first_slot", [P, NE])
        offset = counts_to
        slot_f = sb("slot_f", [P, HT, 2])
        slot_i = sb("slot_i", [P, HALVES, HT, 2], I32)
        owner = centered[0:1].rearrange("p a i d -> p (a i d)")[:, 0:BLOCKS * NE].rearrange("p (n e) -> p n e", e=NE)
        owner_f = sb("owner_f", [1, BLOCKS])
        owner_i = sb("owner_i", [1, HALVES, BLOCKS], I32)
        diff = sb("diff", [P, HALVES, HT])
        expd = sb("expd", [P, HALVES, HT])
        den = sb("den", [P, HALVES, HT])
        weight = sb("weight", [P, HALVES, HT, 2])
        place = dg[:, :, :, :].rearrange("p a j t -> p (a j t)")
        wide, narrow = 2 * GB * P, 2 * GB * D

        def over_dg(at, size, c):
            return place[:, at:at + size].rearrange("p (s n c) -> p s n c", s=2, c=c)

        slots = over_dg(0, wide, 2 * D)
        silu = over_dg(wide, wide, HID)
        act = over_dg(2 * wide, wide, HID)
        act_t = over_dg(3 * wide, wide, P)
        res = over_dg(4 * wide, narrow, D)
        w3_sb = place[:, 4 * wide + narrow:4 * wide + narrow + NE * D]
        slots_t = qk[:, 0, 2, 0:wide].rearrange("p (s n c) -> p s n c", s=2, c=P)
        w12_hi = qk[:, 0, 0:2, :].rearrange("p a n -> p (a n)")
        w12_lo = qk[:, 1, 0:2, :].rearrange("p a n -> p (a n)")
        back_v = x_raw[:, :].rearrange("p (h i k d) -> p h i k d", h=HALVES, k=2, d=D)

        ring = ctx.enter_context(nc.psum_tensor("ring", [P, 4, CW], F32))
        acc = ctx.enter_context(nc.psum_tensor("acc", [P, CW], F32))
        bank5 = ctx.enter_context(nc.psum_tensor("bank5", [P, CW], F32))
        bank6 = ctx.enter_context(nc.psum_tensor("bank6", [P, CW], F32))
        bank7 = ctx.enter_context(nc.psum_tensor("bank7", [P, CW], F32))

        ld_w, ld_vec, ld_wo, ld_wy, ld_w3, ld_w12 = (sem(f"ld_{n}") for n in ("w", "vec", "wo", "wy", "w3", "w12"))
        ld_x = [sem(f"ld_x{i}") for i in range(NB)]
        ld_dg = [sem(f"ld_dg{i}") for i in range(8)]
        zeroed = sem("zeroed")
        consts_pool = sem("consts_pool")
        consts = sem("consts")
        w_split_hi, w_split = sem("w_split_hi"), sem("w_split")
        x_high, x_split = sem("x_high"), sem("x_split")
        proj_done, proj_high, proj_free = sem("proj_done"), sem("proj_high"), sem("proj_free")
        scores_done, mixed_done, pv_done, ret_done = sem("scores_done"), sem("mixed_done"), sem("pv_done"), sem("ret_done")
        y_done, y_read = sem("y_done"), sem("y_read")
        center = [sem("center1"), sem("center2")]
        squared = [sem("squared1"), sem("squared2")]
        var_done = [sem("var1"), sem("var2")]
        std_done = [sem("std1"), sem("std2")]
        norm_done = [sem("norm1"), sem("norm2")]
        high_done = [sem("high1"), sem("high2")]
        rows_done = [sem("rows1"), sem("rows2")]
        turned = [sem("turned1"), sem("turned2")]
        in_done = [sem("in1"), sem("in2")]
        db_done, xc_done, sig_done, b_read = sem("db_done"), sem("xc_done"), sem("sig_done"), sem("b_read")
        xb_done, cb_done = sem("xb_done"), sem("cb_done")
        u_done, scan_done, read_done = sem("u_done"), sem("scan_done"), sem("read_done")
        wy_done, h2_done = sem("wy_done"), sem("h2_done")
        gate_done, logits_done = sem("gate_done"), sem("logits_done")
        chosen_done, count_done, count_read = sem("chosen_done"), sem("count_done"), sem("count_read")
        slot_done, owner_done, diff_done, exp_done = sem("slot_done"), sem("owner_done"), sem("diff_done"), sem("exp_done")
        w12_hi_done, w12_lo_done = sem("w12_hi_done"), sem("w12_lo_done")
        scattered = [sem(f"scattered{i}") for i in range(HALVES)]
        ld_slots = [sem("ld_slots0"), sem("ld_slots1")]
        sturned, sin_done = sem("sturned"), sem("sin_done")
        hid_done, silu_done, act_done = sem("hid_done"), sem("silu_done"), sem("act_done")
        aturned, ain_done = sem("aturned"), sem("ain_done")
        res_done, res_read = sem("res_done"), sem("res_read")
        stored = [sem("stored0"), sem("stored1")]
        gathered = [sem(f"gathered{i}") for i in range(HALVES * COMBINES)]
        combined = sem("combined")
        out_done = sem("out_done")
        dve_step = sem("dve_step")

        block = ctx.enter_context(nc.Block())

        def unit_of(u):
            return u // 2, u % 2

        def cycle(g):
            return (g if g < UNITS else None, g - 1 if 0 <= g - 1 < UNITS else None,
                    g - 2 if 0 <= g - 2 < UNITS else None)

        def load_of_dg(th, j):
            return ld_dg[4 * th + j // 2]

        @block.sync
        def _(sp):
            sp.dma_start(w_raw[:, :], wproj).then_inc(ld_w, 16)
            sp.dma_start(vec[:, :], vecs).then_inc(ld_vec, 16)
            sp.dma_start(row[:, :], rows).then_inc(ld_vec, 16)

            def load_x(b):
                for r in (0, D):
                    sp.dma_start(x_raw[r:r + D, b * T:(b + 1) * T], xT[b]).then_inc(ld_x[b], 16)

            load_x(0)
            load_x(1)
            for th in range(2):
                for jj in range(4):
                    sp.dma_start(dg[:, th, 2 * jj:2 * jj + 2, :],
                                 dgT[2 * jj * P:(2 * jj + 2) * P, th * CW:(th + 1) * CW]
                                 .rearrange("(a p) t -> p a t", p=P)).then_inc(ld_dg[4 * th + jj], 16)
                if th == 0:
                    sp.dma_start(wo_sb[:, :], wo).then_inc(ld_wo, 16)
                    sp.dma_start(wy_sb[:, :], wy).then_inc(ld_wy, 16)
                    load_x(2)
                    load_x(3)
            sp.wait_ge(consts, 1)
            for hh in range(HALVES):
                flat = slots_dram[hh].rearrange("(p a z c) e -> p a z (c e)", p=P, a=ZEROINGS, c=2)
                for i in range(ZEROINGS):
                    sp.dma_start(flat[:, i], zeros[:, :].unsqueeze(1).broadcast_to([P, flat.shape[2], 256])).then_inc(zeroed, 16)
            sp.wait_ge(x_split, NB)
            for r in (0, D):
                sp.dma_start(x_raw[r:r + D, :], w12).then_inc(ld_w12, 16)

            sp.wait_ge(mixed_done, UNITS * STEPS)
            sp.dma_start(w3_sb[:, :], w3).then_inc(ld_w3, 16)

            def load_slots(hh, g):
                n = hh * GROUPS + g
                if g == 0:
                    sp.wait_ge(scattered[hh], 16 * 2 * HT)
                if n >= 2:
                    sp.wait_ge(sturned, n - 1)
                sp.dma_start(slots[:, n % 2, :, :],
                             slots_dram[hh][g * GB * P:(g + 1) * GB * P, :]
                             .rearrange("(n p) c -> p n c", p=P)).then_inc(ld_slots[n % 2], 16)

            def store_results(hh, g):
                n = hh * GROUPS + g
                sp.wait_ge(res_read, n + 1)
                sp.dma_start(results_dram[hh][g * GB * P:(g + 1) * GB * P, :]
                             .rearrange("(n p) c -> p n c", p=P), res[:, n % 2, :, :]).then_inc(stored[n % 2], 16)

            for hh in range(HALVES):
                for g in range(GROUPS + 4):
                    if g < GROUPS:
                        load_slots(hh, g)
                    if g >= 4:
                        store_results(hh, g - 4)

            for hh in range(HALVES):
                for m in range(COMBINES):
                    sp.wait_ge(combined, hh * COMBINES + m + 1)
                    for bb in range(BH):
                        t0 = m * LAST_TILES // BH
                        nt = LAST_TILES // BH
                        sp.dma_start(
                            out[hh * BH + bb, t0 * P:(t0 + nt) * P, :].rearrange("(t p) d -> p t d", p=P),
                            h[:, hh, :, :].rearrange("p (t b) d -> p t b d", b=BH)[:, t0:t0 + nt, bb, :]
                        ).then_inc(out_done, 16)
            sp.wait_ge(out_done, 16 * HALVES * COMBINES * BH)

        @block.gpsimd
        def _(pool):
            n = [0]

            def link(ins):
                n[0] += 1
                ins.then_inc(consts_pool, 1)
                pool.wait_ge(consts_pool, n[0])

            link(pool.memset(zeros[:, :], 0.0))
            link(pool.memset(ident[:, :], 0.0))
            link(pool.affine_select(out=ident[:, :], in_=ident[:, :], compare_op=ALU.not_equal, fill=1.0,
                                    base=0, pattern=[[-1, P]], channel_multiplier=1))
            link(pool.memset(ones[:, :], 1.0))
            link(pool.affine_select(out=before[:, :], in_=ones[:, :], compare_op=ALU.is_gt, fill=0.0,
                                    base=0, pattern=[[1, P]], channel_multiplier=-1))
            link(pool.memset(eps[:, :], EPS))
            link(pool.memset(ones16[:, :], 1.0))
            link(pool.memset(not_first[:, :, :], 1.0))
            link(pool.memset(not_first[:, :, 0:1], 0.0))
            link(pool.iota(iota_i[:, 0:NE], [[-1, NE]], NE, 0))
            link(pool.tensor_copy(rank_of[:, :], iota_i[:, 0:NE]))
            link(pool.iota(iota_i[:, :], [[1, BLOCKS]], 0, 0))
            pool.tensor_copy(block_no[:, :], iota_i[0:1, :]).then_inc(consts, 1)

            pool.wait_ge(scores_done, UNITS * STEPS)
            for i in range(4):
                c = slice(i * 1024, (i + 1) * 1024)
                pool.wait_ge(w12_hi_done, i + 1)
                pool.tensor_tensor(w12_lo[:, c], x_raw[:, c], w12_hi[:, c], ALU.subtract).then_inc(w12_lo_done, 1)

            def scatter(hh):
                pool.wait_ge(zeroed, 16 * HALVES * ZEROINGS)
                pool.wait_ge(rows_done[1], 2 * hh + 2)
                pool.wait_ge(slot_done, hh + 1)
                for i in range(HT):
                    for k in range(2):
                        pool.indirect_dma_start(
                            out=slots_dram[hh], out_offset=bass.IndirectOffsetOnAxis(ap=slot_i[:, hh, i, k:k + 1], axis=0),
                            in_=ffn_rows[:, hh, i, :], in_offset=None).then_inc(scattered[hh], 16)

            def gather(hh):
                n0 = hh * GROUPS
                for s in range(2):
                    pool.wait_ge(stored[s], 16 * ((n0 + GROUPS) // 2))
                if hh == 0:
                    pool.wait_ge(w12_lo_done, 4)
                for m in range(COMBINES):
                    for i in range(m * LAST_TILES, (m + 1) * LAST_TILES):
                        for k in range(2):
                            pool.indirect_dma_start(
                                out=back_v[:, hh, i, k, :], out_offset=None, in_=results_dram[hh],
                                in_offset=bass.IndirectOffsetOnAxis(ap=slot_i[:, hh, i, k:k + 1], axis=0)
                            ).then_inc(gathered[hh * COMBINES + m], 16)

            scatter(0)
            scatter(1)
            gather(0)
            gather(1)

        @block.scalar
        def _(s):
            def projections(hh):
                for use in range(2, 10):
                    b, kind, th = (use - 2) // 4, (use - 2) % 4 // 2, use % 2
                    s.wait_ge(proj_done, 10 * hh + use + 1)
                    dst = qk[:, hh, 1 if kind == 0 else 0, b * T + th * CW:b * T + (th + 1) * CW]
                    s.activation(dst, ring[:, use % 4, :], ACT.Identity,
                                 bias=vec[:, (BK if kind == 0 else BQ):(BK if kind == 0 else BQ) + 1]).then_inc(proj_high, 1)

            def norm_squares(which, u):
                s.wait_ge(center[which], u + 1)
                if u >= 1:
                    s.wait_ge(var_done[which], u)
                s.activation(squares[:, which], centered[:, which], ACT.Square).then_inc(squared[which], 1)

            def norm_std(which, u):
                s.wait_ge(var_done[which], u + 1)
                s.activation(stats[:, which, 3, :], stats[:, which, 2, :], ACT.Sqrt, scale=1.0 / D,
                             bias=eps[:, 0:1]).then_inc(std_done[which], 1)

            def rows_of(which, u):
                hh, c = unit_of(u)
                return ssm_rows[:, :, :] if which == 0 else ffn_rows[:, hh, c * UT:(c + 1) * UT, :]

            def norm_high(which, u):
                s.wait_ge(norm_done[which], u + 1)
                if which == 0 and u >= 1:
                    s.wait_ge(turned[0], 2 * u)
                s.activation(rows_of(which, u)[:, :, 0:D].bitcast(F32R), normed[:, which], ACT.Copy).then_inc(high_done[which], 1)

            def take_turned(which, u):
                dst = ssm_in if which == 0 else gate_in
                for b in range(BH):
                    s.wait_ge(turned[which], 2 * u + b + 1)
                    if u >= 1:
                        if which == 0:
                            s.wait_ge(xc_done, 2 * u)
                        else:
                            s.wait_ge(gate_done, u)
                    s.activation(dst[:, b, :], (bank6, bank7)[b][:, :], ACT.Copy).then_inc(in_done[which], 1)

            def sigmoids(u, b):
                w = 2 * u + b
                s.wait_ge(db_done, w + 1)
                if w >= 2:
                    s.wait_ge(scan_done, w - 1)
                s.activation(take[:, w % 2, :], bank6[:, :], ACT.Sigmoid, bias=vec[:, BD:BD + 1]).then_inc(sig_done, 1)
                s.activation(keep[:, w % 2, :], bank6[:, :], ACT.Sigmoid, scale=-1.0, bias=neg_bd[:, 0:1]).then_inc(sig_done, 1)

            def x_and_c(u, b):
                w = 2 * u + b
                s.wait_ge(xc_done, w + 1)
                if w >= 2:
                    s.wait_ge(u_done, w - 1)
                    s.wait_ge(wy_done, u)
                s.activation(xb[:, w % 2, :], bank7[:, :], ACT.Identity, bias=vec[:, BX:BX + 1]).then_inc(xb_done, 1)
                s.activation(cb[:, w % 2, :], bank6[:, :], ACT.Identity, bias=vec[:, BC:BC + 1]).then_inc(cb_done, 1)

            s.wait_ge(ld_w, 16)
            s.activation(w_hi[:, :], w_raw[:, :], ACT.Copy).then_inc(w_split_hi, 1)

            def x_highs(hh):
                for b in range(hh * BH, (hh + 1) * BH):
                    s.wait_ge(ld_x[b], 32)
                    if b == BH:
                        s.wait_ge(proj_done, 10)
                    c = b % BH * T
                    s.activation(x_parts[:, c:c + T], x_raw[:, b * T:(b + 1) * T], ACT.Copy).then_inc(x_high, 1)

            x_highs(0)
            s.wait_ge(ld_vec, 32)
            projections(0)
            s.wait_ge(consts, 1)
            for g in range(UNITS + 2):
                mix, first, second = cycle(g)
                if g == 1:
                    x_highs(1)
                if g == 2:
                    projections(1)
                if second is not None:
                    norm_squares(1, second)
                if first is not None:
                    norm_squares(0, first)
                if second is not None:
                    norm_std(1, second)
                if first is not None:
                    norm_std(0, first)
                if second is not None:
                    norm_high(1, second)
                if first is not None:
                    norm_high(0, first)
                if second is not None:
                    take_turned(1, second)
                if first is not None:
                    take_turned(0, first)
                    sigmoids(first, 0)
                    x_and_c(first, 0)
                    sigmoids(first, 1)
                    x_and_c(first, 1)
                if g == 2:
                    s.wait_ge(ld_w12, 32)
                    s.wait_ge(scores_done, 2 * STEPS)
                    for i in range(4):
                        c = slice(i * 1024, (i + 1) * 1024)
                        s.activation(w12_hi[:, c], x_raw[:, c], ACT.Copy).then_inc(w12_hi_done, 1)
                if second is not None and second % 2 == 1:
                    hh = second // 2
                    s.wait_ge(diff_done, hh + 1)
                    s.activation(expd[:, hh, :], diff[:, hh, :], ACT.Exp).then_inc(exp_done, 1)
                if mix is not None:
                    s.wait_ge(pv_done, (mix + 1) * STEPS)
                    if mix >= 1:
                        s.wait_ge(y_done, mix)
                    s.activation(ret[:, :], acc[:, :], ACT.Copy).then_inc(ret_done, 1)

            def take_slots(n):
                s.wait_ge(sturned, n + 1)
                if n >= 2:
                    s.wait_ge(hid_done, n - 1)
                s.activation(slots_t[:, n % 2].rearrange("p n c -> p (n c)"), ring[:, 0, :], ACT.Copy).then_inc(sin_done, 1)

            def silus(n):
                s.wait_ge(hid_done, n + 1)
                if n >= 2:
                    s.wait_ge(act_done, n - 1)
                h1 = ring[:, 1:3, :].rearrange("p a (n c) -> p (a n) c", c=2 * HID)[:, :, 0:HID]
                s.activation(silu[:, n % 2], h1, ACT.Silu).then_inc(silu_done, 1)

            def take_act(n):
                s.wait_ge(aturned, n + 1)
                if n >= 2:
                    s.wait_ge(res_done, n - 1)
                s.activation(act_t[:, n % 2].rearrange("p n c -> p (n c)"), ring[:, 3, :], ACT.Copy).then_inc(ain_done, 1)

            for hh in range(HALVES):
                for g in range(GROUPS + 2):
                    if g < GROUPS:
                        take_slots(hh * GROUPS + g)
                    if 1 <= g <= GROUPS:
                        silus(hh * GROUPS + g - 1)
                    if g >= 2:
                        take_act(hh * GROUPS + g - 2)

        @block.tensor
        def _(pe):
            def split_product(dst, moving, lo_col, n, last=True):
                pe.matmul(dst, w_hi[:, lo_col:lo_col + n], moving, start=True, stop=False)
                return pe.matmul(dst, w_lo[:, lo_col:lo_col + n], moving, start=False, stop=True)

            def projections(hh):
                pe.wait_ge(w_split, 1)
                if hh:
                    pe.wait_ge(mixed_done, 2 * STEPS)
                for use in range(10):
                    if use >= 4:
                        pe.wait_ge(proj_free, 10 * hh + use - 3)
                    if use < 2:
                        b = use
                        pe.wait_ge(x_split, hh * BH + b + 1)
                        for j in range(JT):
                            x0 = b * T + j * P
                            for part, w in enumerate((w_hi, w_lo)):
                                mm = pe.matmul(ring[:, use, j * D:(j + 1) * D], x_parts[:, x0:x0 + P],
                                               w[:, V0:V0 + D], start=part == 0, stop=part == 1)
                    else:
                        b, kind, th = (use - 2) // 4, (use - 2) % 4 // 2, use % 2
                        x0 = b * T + th * CW
                        mm = split_product(ring[:, use % 4, :], x_parts[:, x0:x0 + CW], K0 if kind == 0 else Q0, P)
                    mm.then_inc(proj_done, 1)

            def scores(u, j):
                m = u * STEPS + j
                hh, th = unit_of(u)
                if j == 0:
                    pe.wait_ge(proj_free, 10 * hh + 10)
                if m >= 2:
                    pe.wait_ge(mixed_done, m - 1)
                for b in range(BH):
                    for part in range(2):
                        mm = pe.matmul(ring[:, 2 * (m % 2) + b, :], qk[:, hh, 1 + part, b * T + j * P:b * T + (j + 1) * P],
                                       qk[:, hh, 0, b * T + th * CW:b * T + (th + 1) * CW],
                                       start=part == 0, stop=part == 1)
                mm.then_inc(scores_done, 1)

            def pv(u, j):
                m = u * STEPS + j
                hh, th = unit_of(u)
                pe.wait_ge(mixed_done, m + 1)
                if j == 0 and u >= 1:
                    pe.wait_ge(ret_done, u)
                for b in range(BH):
                    mm = pe.matmul(acc[b * D:(b + 1) * D, :], v[:, hh, b, j, :], mixed[:, m % 2, b, :],
                                   start=j == 0, stop=j == JT - 1)
                mm.then_inc(pv_done, 1)

            def y_product(u):
                pe.wait_ge(ret_done, u + 1)
                if u == 0:
                    pe.wait_ge(ld_wo, 16)
                else:
                    pe.wait_ge(h2_done, u)
                    pe.wait_ge(xb_done, 2 * u)
                for i in range(UT):
                    b, t = i % BH, i // BH
                    mm = pe.matmul((bank5, bank7)[b][:, t * D:(t + 1) * D], ret[b * D:(b + 1) * D, t * P:(t + 1) * P],
                                   wo_sb[b * D:(b + 1) * D, :], start=True, stop=True)
                mm.then_inc(y_done, 1)

            def turn_rows(which, u):
                hh, c = unit_of(u)
                rows_ = ssm_rows[:, :, :] if which == 0 else ffn_rows[:, hh, c * UT:(c + 1) * UT, :]
                pe.wait_ge(rows_done[which], u + 1)
                if which == 0 and u >= 1:
                    pe.wait_ge(in_done[1], 2 * u)
                pe.wait_ge(y_read, 2 * min(u + 1 + which, UNITS))
                if which == 1:
                    pe.wait_ge(xb_done, 2 * u + 2)
                    pe.wait_ge(cb_done, 2 * u + 2)
                for b in range(BH):
                    for t in range(UT // BH):
                        mm = pe.transpose((bank6, bank7)[b][:, t * P:(t + 1) * P], rows_[:, t * BH + b, :], ident[:, :])
                    mm.then_inc(turned[which], 1)

            def delta_and_b(u, b):
                w = 2 * u + b
                pe.wait_ge(in_done[0], 2 * u + 2)
                if b == 1:
                    pe.wait_ge(cb_done, w)
                    pe.wait_ge(xb_done, w)
                split_product(bank6[:, :], ssm_in[:, b, :], D0, CH)
                split_product(bank7[:, :], ssm_in[:, b, :], B0, CH).then_inc(db_done, 1)

            def x_and_c(u, b):
                w = 2 * u + b
                pe.wait_ge(b_read, w + 1)
                split_product(bank7[:, :], ssm_in[:, b, :], X0, CH)
                pe.wait_ge(sig_done, 2 * w + 2)
                split_product(bank6[:, :], ssm_in[:, b, :], C0, CH).then_inc(xc_done, 1)

            def ssm_out(u):
                if u == 0:
                    pe.wait_ge(ld_wy, 16)
                    pe.wait_ge(y_read, 2)
                else:
                    pe.wait_ge(logits_done, u)
                    if u % 2 == 0:
                        pe.wait_ge(count_read, u // 2)
                pe.wait_ge(read_done, 2 * u + 2)
                for i in range(UT):
                    b, t = i % BH, i // BH
                    mm = pe.matmul(bank5[:, i * D:(i + 1) * D], read[:, b, t * P:(t + 1) * P], wy_sb[:, :],
                                   start=True, stop=True)
                mm.then_inc(wy_done, 1)

            def gate(u):
                pe.wait_ge(in_done[1], 2 * u + 2)
                pe.wait_ge(y_read, 2 * min(u + 2, UNITS))
                pe.wait_ge(h2_done, u + 1)
                for i in range(UT):
                    b, t = i % BH, i // BH
                    for part, w in enumerate((w_hi, w_lo)):
                        mm = pe.matmul(bank5[:, i * NE:(i + 1) * NE], gate_in[:, b, t * P:(t + 1) * P],
                                       w[:, G0:G0 + NE], start=part == 0, stop=part == 1)
                mm.then_inc(gate_done, 1)

            def count(hh):
                pe.wait_ge(chosen_done, hh + 1)
                picked = chosen[:, :, :].rearrange("p i e -> p (i e)")
                pe.matmul(bank5[:, 0:HT * NE], before[:, :], picked, start=True, stop=True)
                pe.matmul(bank5[:, HT * NE:2 * HT * NE], ones[:, :], picked, start=True, stop=True).then_inc(count_done, 1)

            projections(0)
            pe.wait_ge(consts, 1)
            for g in range(UNITS + 2):
                mix, first, second = cycle(g)
                if g == 2:
                    projections(1)
                for j in range(STEPS):
                    if mix is not None:
                        scores(mix, j)
                        if j >= 1:
                            pv(mix, j - 1)
                    if j == 0 and second is not None:
                        ssm_out(second)
                    if j == 0 and first is not None:
                        y_product(first)
                    if j == 4 and second is not None:
                        turn_rows(1, second)
                    if j == 4 and first is not None:
                        turn_rows(0, first)
                    if j == 5 and second is not None:
                        gate(second)
                    if j == 5 and first is not None:
                        delta_and_b(first, 0)
                    if j == 6 and second is not None and second % 2 == 1:
                        count(second // 2)
                    if j == 6 and first is not None:
                        x_and_c(first, 0)
                        delta_and_b(first, 1)
                    if j == 7 and first is not None:
                        x_and_c(first, 1)
                if mix is not None:
                    pv(mix, JT - 1)

            experts = {}

            def turn_slots(hh, g):
                n = hh * GROUPS + g
                pe.wait_ge(ld_slots[n % 2], 16 * (n // 2 + 1))
                if n >= 1:
                    pe.wait_ge(sin_done, n)
                for k in range(GB):
                    mm = pe.transpose(ring[:, 0, k * P:(k + 1) * P], slots[:, n % 2, k, :], ident[:, :])
                mm.then_inc(sturned, 1)

            def hidden(hh, g):
                n = hh * GROUPS + g
                if g == 0:
                    pe.wait_ge(owner_done, hh + 1)
                if n == 0:
                    pe.wait_ge(w12_lo_done, 4)
                _, experts[n] = nc.values_load_multi_w_load_instructions(
                    owner_i[0:1, hh, g * GB:(g + 1) * GB], engines=[PE_ENGINE], min_val=0, max_val=NE - 1,
                    skip_runtime_bounds_check_because="the owner of a block is at most NE - 1")
                pe.wait_ge(sin_done, n + 1)
                if n >= 1:
                    pe.wait_ge(act_done, n)
                for k in range(GB):
                    for part, w in enumerate((w12_hi, w12_lo)):
                        mm = pe.matmul(ring[:, 1 + k // 2, k % 2 * 2 * HID:(k % 2 + 1) * 2 * HID], slots_t[:, n % 2, k, :],
                                       w[:, bass.ds(experts[n][k] * (2 * HID), 2 * HID)], start=part == 0, stop=part == 1)
                mm.then_inc(hid_done, 1)

            def turn_act(n):
                pe.wait_ge(act_done, n + 1)
                if n >= 1:
                    pe.wait_ge(ain_done, n)
                for k in range(GB):
                    mm = pe.transpose(ring[:, 3, k * P:(k + 1) * P], act[:, n % 2, k, :], ident[:, :])
                mm.then_inc(aturned, 1)

            def result(n):
                if n == 0:
                    pe.wait_ge(ld_w3, 16)
                    pe.wait_ge(ret_done, UNITS)
                else:
                    pe.wait_ge(res_read, n)
                pe.wait_ge(ain_done, n + 1)
                for k in range(GB):
                    mm = pe.matmul(acc[:, k * D:(k + 1) * D], act_t[:, n % 2, k, :],
                                   w3_sb[:, bass.ds(experts[n][k] * D, D)], start=True, stop=True)
                mm.then_inc(res_done, 1)

            pe.wait_ge(mixed_done, UNITS * STEPS)
            for hh in range(HALVES):
                for g in range(GROUPS + 3):
                    if g < GROUPS:
                        turn_slots(hh, g)
                    if 1 <= g <= GROUPS:
                        hidden(hh, g - 1)
                    if 2 <= g <= GROUPS + 1:
                        turn_act(hh * GROUPS + g - 2)
                    if g >= 3:
                        result(hh * GROUPS + g - 3)

        @block.vector
        def _(dve):
            steps = [0]

            def link(ins):
                steps[0] += 1
                ins.then_inc(dve_step, 1)
                dve.wait_ge(dve_step, steps[0])

            def row_of(c0, n, shape):
                return row[:, c0:c0 + n].unsqueeze(1).broadcast_to(shape)

            def x_lows(hh):
                for b in range(hh * BH, (hh + 1) * BH):
                    dve.wait_ge(x_high, b + 1)
                    c = slice(b % BH * T, (b % BH + 1) * T)
                    dve.tensor_tensor(x_parts[D:P, c], x_raw[D:P, b * T:(b + 1) * T], x_parts[D:P, c],
                                      ALU.subtract).then_inc(x_split, 1)

            def projections(hh):
                for use in range(10):
                    if use < 2:
                        dve.wait_ge(proj_done, 10 * hh + use + 1)
                        dve.tensor_tensor(v[:, hh, use], ring[:, use, :].rearrange("p (j d) -> p j d", d=D),
                                          row_of(RV, D, [P, JT, D]), ALU.add).then_inc(proj_free, 1)
                        continue
                    b, kind, th = (use - 2) // 4, (use - 2) % 4 // 2, use % 2
                    c = slice(b * T + th * CW, b * T + (th + 1) * CW)
                    dve.wait_ge(proj_high, 8 * hh + use - 1)
                    r = slice(0, P) if kind == 0 else slice(D, P)
                    dve.scalar_tensor_tensor(out=qk[r, hh, 2 if kind == 0 else 0, c], in0=ring[r, use % 4, :],
                                             scalar=vec[r, (BK if kind == 0 else BQ):(BK if kind == 0 else BQ) + 1],
                                             in1=qk[r, hh, 1 if kind == 0 else 0, c], op0=ALU.add, op1=ALU.subtract
                                             ).then_inc(proj_free, 1)

            def mix_step(u, j):
                m = u * STEPS + j
                hh, th = unit_of(u)
                if u < 2 and j % 2 == 0:
                    dve.wait_ge(load_of_dg(th, j), 16)
                dve.wait_ge(scores_done, m + 1)
                if m >= 2:
                    dve.wait_ge(pv_done, m - 1)
                dve.tensor_tensor(mixed[:, m % 2], ring[:, 2 * (m % 2):2 * (m % 2) + 2, :],
                                  dg[:, th, j, :].unsqueeze(1).broadcast_to([P, BH, CW]), ALU.mult).then_inc(mixed_done, 1)

            def unit_h(u):
                hh, c = unit_of(u)
                return h[:, hh, c * UT:(c + 1) * UT, :]

            def prelu(u):
                dve.wait_ge(y_done, u + 1)
                hu = unit_h(u)
                for b in range(BH):
                    dve.tensor_tensor(hu.rearrange("p (t b) d -> p t b d", b=BH)[:, :, b, :],
                                      (bank5, bank7)[b][:, 0:UT // BH * D].rearrange("p (t d) -> p t d", d=D),
                                      row_of(RO, D, [P, UT // BH, D]), ALU.add).then_inc(y_read, 1)
                dve.wait_ge(y_read, 2 * u + 2)
                link(dve.tensor_scalar(prelu_neg, hu, 0.0, vec[:, PRELU:PRELU + 1], ALU.min, ALU.mult))
                link(dve.scalar_tensor_tensor(out=hu, in0=hu, scalar=0.0, in1=prelu_neg, op0=ALU.max, op1=ALU.add))

            def norm_center(which, u):
                hu = unit_h(u)
                link(dve.tensor_reduce(stats[:, which, 0, :], hu, AX_X, ALU.add))
                link(dve.tensor_scalar(stats[:, which, 1, :], stats[:, which, 0, :], -1.0 / D, None, ALU.mult))
                dve.tensor_tensor(centered[:, which], hu, stats[:, which, 1, :].unsqueeze(2).broadcast_to([P, UT, D]),
                                  ALU.add).then_inc(center[which], 1)

            def norm_var(which, u):
                dve.wait_ge(squared[which], u + 1)
                dve.tensor_reduce(stats[:, which, 2, :], squares[:, which], AX_X, ALU.add).then_inc(var_done[which], 1)

            def norm_scale(which, u):
                dve.wait_ge(std_done[which], u + 1)
                link(dve.reciprocal(stats[:, which, 4, :], stats[:, which, 3, :]))
                if u >= 1:
                    dve.wait_ge(high_done[which], u)
                dve.tensor_tensor(normed[:, which], centered[:, which],
                                  stats[:, which, 4, :].unsqueeze(2).broadcast_to([P, UT, D]), ALU.mult).then_inc(norm_done[which], 1)

            def norm_low(which, u):
                hh, c = unit_of(u)
                rows_ = ssm_rows[:, :, :] if which == 0 else ffn_rows[:, hh, c * UT:(c + 1) * UT, :]
                dve.wait_ge(high_done[which], u + 1)
                dve.tensor_tensor(rows_[:, :, D:2 * D], normed[:, which], rows_[:, :, 0:D], ALU.subtract).then_inc(rows_done[which], 1)

            def ssm_b(u, b):
                w = 2 * u + b
                dve.wait_ge(sig_done, 2 * w + 2)
                dve.scalar_tensor_tensor(out=drive[:, w % 2, :], in0=bank7[:, :], scalar=vec[:, BB:BB + 1],
                                         in1=take[:, w % 2, :], op0=ALU.add, op1=ALU.mult).then_inc(b_read, 1)

            def ssm_scan(u, b):
                w = 2 * u + b
                _, c = unit_of(u)
                dve.wait_ge(xb_done, w + 1)
                dve.wait_ge(b_read, w + 1)
                dve.tensor_tensor(drive[:, w % 2, :], drive[:, w % 2, :], xb[:, w % 2, :], ALU.mult).then_inc(u_done, 1)
                dve.wait_ge(u_done, w + 1)
                start = 0.0 if c == 0 else state[:, b, 0, CW - 1:CW]
                dve.tensor_tensor_scan(state[:, b, c, :], keep[:, w % 2, :], drive[:, w % 2, :], start,
                                       ALU.mult, ALU.add).then_inc(scan_done, 1)
                dve.wait_ge(scan_done, w + 1)
                dve.wait_ge(cb_done, w + 1)
                dve.tensor_tensor(read[:, b, :], state[:, b, c, :], cb[:, w % 2, :], ALU.mult).then_inc(read_done, 1)

            def residual(u):
                hu = unit_h(u)
                dve.wait_ge(wy_done, u + 1)
                dve.tensor_tensor(hu, bank5[:, :].rearrange("p (i d) -> p i d", d=D), hu, ALU.add).then_inc(h2_done, 1)
                dve.wait_ge(h2_done, u + 1)
                link(dve.tensor_tensor(hu, hu, row_of(RY, D, [P, UT, D]), ALU.add))

            def take_logits(u):
                hh, c = unit_of(u)
                dve.wait_ge(gate_done, u + 1)
                dve.tensor_tensor(logits[:, c * UT:(c + 1) * UT, :],
                                  bank5[:, 0:UT * NE].rearrange("p (i e) -> p i e", e=NE),
                                  row_of(RG, NE, [P, UT, NE]), ALU.add).then_inc(logits_done, 1)

            def route(hh):
                full = [P, HT, NE]
                lg = logits[:, :, :]
                dve.wait_ge(logits_done, 2 * hh + 2)
                for k in range(2):
                    link(dve.tensor_reduce(best[:, hh, k, :], lg, AX_X, ALU.max))
                    link(dve.tensor_tensor(r_a[:, :, :], lg, best[:, hh, k, :].unsqueeze(2).broadcast_to(full), ALU.is_equal))
                    link(dve.tensor_tensor(r_a[:, :, :], r_a[:, :, :], rank_of[:, :].unsqueeze(1).broadcast_to(full), ALU.mult))
                    link(dve.tensor_reduce(r_b[:, :], r_a[:, :, :], AX_X, ALU.max))
                    link(dve.tensor_tensor(top[:, k], r_a[:, :, :], r_b[:, :].unsqueeze(2).broadcast_to(full), ALU.is_equal))
                    if k == 0:
                        link(dve.scalar_tensor_tensor(out=lg, in0=top[:, 0], scalar=-3e38, in1=lg,
                                                      op0=ALU.mult, op1=ALU.add))
                dve.tensor_tensor(chosen[:, :, :], top[:, 0], top[:, 1], ALU.add).then_inc(chosen_done, 1)
                dve.tensor_tensor(diff[:, hh, :], best[:, hh, 1, :], best[:, hh, 0, :], ALU.subtract).then_inc(diff_done, 1)
                dve.wait_ge(count_done, hh + 1)
                in_tile = bank5[:, HT * NE:2 * HT * NE].rearrange("p (i e) -> p e i", e=NE)
                link(dve.tensor_copy(counts[:, :, :], in_tile))
                link(dve.tensor_tensor_scan(counts_to[:, :, :].rearrange("p e i -> p (e i)"),
                                            not_first[:, :, :].rearrange("p e i -> p (e i)"),
                                            counts[:, :, :].rearrange("p e i -> p (e i)"), 0.0, ALU.mult, ALU.add))
                link(dve.tensor_scalar(n_int[:, :], counts_to[:, :, HT - 1], float(P - 1), None, ALU.add))
                link(dve.tensor_scalar(n_int[:, :], n_int[:, :], 7, None, ALU.logical_shift_right))
                link(dve.tensor_copy(n_blocks[:, :], n_int[:, :]))
                link(dve.tensor_tensor_scan(blocks_to[:, :], ones16[:, :], n_blocks[:, :], 0.0, ALU.mult, ALU.add))
                link(dve.tensor_tensor(first_slot[:, :], blocks_to[:, :], n_blocks[:, :], ALU.subtract))
                link(dve.tensor_tensor(offset[:, :, :], counts_to[:, :, :], counts[:, :, :], ALU.subtract))
                link(dve.scalar_tensor_tensor(out=offset[:, :, :], in0=first_slot[:, :].unsqueeze(2).broadcast_to([P, NE, HT]),
                                              scalar=float(P), in1=offset[:, :, :], op0=ALU.mult, op1=ALU.add))
                dve.tensor_tensor(slot[:, :, :], bank5[:, 0:HT * NE].rearrange("p (i e) -> p i e", e=NE),
                                  offset[:, :, :].rearrange("p e i -> p i e"), ALU.add).then_inc(count_read, 1)
                dve.wait_ge(count_read, hh + 1)
                for k in range(2):
                    link(dve.tensor_tensor(r_a[:, :, :], slot[:, :, :], top[:, k], ALU.mult))
                    link(dve.tensor_reduce(slot_f[:, :, k], r_a[:, :, :], AX_X, ALU.add))
                dve.tensor_copy(slot_i[:, hh], slot_f[:, :, :]).then_inc(slot_done, 1)

            def owners(hh):
                link(dve.tensor_tensor(owner[:, :, :], blocks_to[0:1, :].unsqueeze(1).broadcast_to([1, BLOCKS, NE]),
                                       block_no[:, :].unsqueeze(2).broadcast_to([1, BLOCKS, NE]), ALU.is_le))
                link(dve.tensor_reduce(owner_f[:, :], owner[:, :, :], AX_X, ALU.add))
                link(dve.tensor_scalar(owner_f[:, :], owner_f[:, :], float(NE - 1), None, ALU.min))
                dve.tensor_copy(owner_i[:, hh, :], owner_f[:, :]).then_inc(owner_done, 1)

            def weights(hh):
                dve.wait_ge(exp_done, hh + 1)
                link(dve.tensor_scalar(den[:, hh, :], expd[:, hh, :], 1.0, None, ALU.add))
                link(dve.reciprocal(weight[:, hh, :, 0], den[:, hh, :]))
                link(dve.tensor_tensor(weight[:, hh, :, 1], expd[:, hh, :], weight[:, hh, :, 0], ALU.mult))

            dve.wait_ge(w_split_hi, 1)
            dve.tensor_tensor(w_lo[:, :], w_raw[:, :], w_hi[:, :], ALU.subtract).then_inc(w_split, 1)
            x_lows(0)
            dve.wait_ge(ld_vec, 32)
            link(dve.tensor_scalar(neg_bd[:, :], vec[:, BD:BD + 1], -1.0, None, ALU.mult))
            projections(0)
            dve.wait_ge(consts, 1)
            for g in range(UNITS + 2):
                mix, first, second = cycle(g)
                if g == 2:
                    projections(1)
                for j in range(STEPS):
                    if mix is not None:
                        mix_step(mix, j)
                    if g == 1 and j == 0:
                        x_lows(1)
                    if j == 0 and second is not None:
                        residual(second)
                    if j == 0 and first is not None:
                        prelu(first)
                    for u, which in ((second, 1), (first, 0)):
                        if u is None:
                            continue
                        if j == 1:
                            norm_center(which, u)
                        if j == 2:
                            norm_var(which, u)
                        if j == 3:
                            norm_scale(which, u)
                    if j == 3:
                        for u, which in ((second, 1), (first, 0)):
                            if u is not None:
                                norm_low(which, u)
                    if j == 5 and second is not None:
                        take_logits(second)
                    if j == 5 and first is not None:
                        ssm_b(first, 0)
                    if j == 6 and second is not None and second % 2 == 1:
                        route(second // 2)
                    if j == 6 and first is not None:
                        ssm_scan(first, 0)
                        ssm_b(first, 1)
                    if j == 7 and first is not None:
                        ssm_scan(first, 1)
                    if j == 7 and second is not None and second % 2 == 1:
                        owners(second // 2)
            weights(0)
            weights(1)

            def gated(n):
                dve.wait_ge(silu_done, n + 1)
                if n >= 2:
                    dve.wait_ge(aturned, n - 1)
                h2 = ring[:, 1:3, :].rearrange("p a (n c) -> p (a n) c", c=2 * HID)[:, :, HID:2 * HID]
                dve.tensor_tensor(act[:, n % 2], h2, silu[:, n % 2], ALU.mult).then_inc(act_done, 1)

            def take_result(n):
                dve.wait_ge(res_done, n + 1)
                if n >= 2:
                    dve.wait_ge(stored[n % 2], 16 * (n // 2))
                dve.tensor_copy(res[:, n % 2], acc[:, 0:GB * D].rearrange("p (n d) -> p n d", d=D)).then_inc(res_read, 1)

            for hh in range(HALVES):
                for g in range(1, GROUPS + 3):
                    if g <= GROUPS:
                        gated(hh * GROUPS + g - 1)
                    if g >= 3:
                        take_result(hh * GROUPS + g - 3)

            for hh in range(HALVES):
                for m in range(COMBINES):
                    i = slice(m * LAST_TILES, (m + 1) * LAST_TILES)
                    dve.wait_ge(gathered[hh * COMBINES + m], 16 * 2 * LAST_TILES)
                    got = back_v[:, hh, i]
                    link(dve.tensor_tensor(got, got, weight[:, hh, i, :].unsqueeze(3).broadcast_to([P, LAST_TILES, 2, D]), ALU.mult))
                    link(dve.tensor_tensor(h[:, hh, i], h[:, hh, i], got[:, :, 0, :], ALU.add))
                    dve.tensor_tensor(h[:, hh, i], h[:, hh, i], got[:, :, 1, :], ALU.add).then_inc(combined, 1)


def kernel(**inputs):
    import numpy as np
    import concourse.bacc as bacc
    from concourse.bass_utils import run_bass_kernel_spmd as run

    def a(name):
        return np.asarray(inputs[name])

    def both(m):
        return np.concatenate([m, m], axis=0)

    wq, wk, wbc = a("L0_tok_Wq"), a("L0_tok_Wk"), a("L0_attn_Wbc")
    n = wbc.shape[1] // 2
    bbc = a("L0_attn_bbc")
    wproj = both(np.concatenate([wq, wq, wk, wk, a("L0_tok_Wv"), a("L0_attn_Wx"), wbc[:, :n], wbc[:, n:],
                                 a("L0_attn_Wd"), a("L0_ffn_gate_w")], axis=1))
    vecs = np.stack([both(a("L0_tok_bq")), both(a("L0_tok_bk")), a("L0_attn_bx"), bbc[:n], bbc[n:], a("L0_attn_bd"),
                     np.broadcast_to(a("L0_tok_prelu_a"), (P,))], axis=1)
    rows = np.broadcast_to(np.concatenate([a("L0_tok_bv"), a("L0_tok_bo"), a("L0_attn_by"), a("L0_ffn_gate_b")]), (P, NROW))
    w12 = np.concatenate([a("L0_ffn_w1"), a("L0_ffn_w2")], axis=2).transpose(1, 0, 2).reshape(D, -1)
    arrays = {
        "xT": a("x").reshape(NB, T, D).transpose(0, 2, 1),
        "dgT": a("L0_tok_d_gamma_batched").T,
        "wproj": wproj, "vecs": vecs, "rows": rows,
        "wo": both(a("L0_tok_Wo")), "wy": a("L0_attn_Wy"), "w12": w12,
        "w3": a("L0_ffn_w3").transpose(1, 0, 2).reshape(HID, -1),
    }
    arrays = {k: np.ascontiguousarray(m) for k, m in arrays.items()}
    nc = bacc.Bacc("TRN2", target_bir_lowering=False, num_devices=1)
    args = [nc.dram_tensor(k, m.shape, mybir.dt.from_np(m.dtype), kind="ExternalInput").ap() for k, m in arrays.items()]
    out = nc.dram_tensor("out", (NB, T, D), F32, kind="ExternalOutput").ap()
    build_layer(nc, *args, out)
    r = run(nc, [arrays], core_ids=[0])
    return r.results[0]["out"]
```

```python
from contextlib import ExitStack

import concourse.bass as bass
from concourse import mybir

F32 = mybir.dt.float32
F32R = mybir.dt.float32r
BF16 = mybir.dt.bfloat16
I32 = mybir.dt.int32
ALU = mybir.AluOpType
ACT = mybir.ActivationFunctionType
AX_X = mybir.AxisListType.X
PE_ENGINE = mybir.EngineType.PE

P = 128
NB, T, D = 4, 1024, 64
CH = 128
NE, HID = 16, 128
HALVES, UNITS = 2, 4
BH = NB // HALVES
CW = T // 2
JT = T // P
UT = BH * CW // P
HT = 2 * UT
STEPS = JT
PART_UNITS = ((0, 1), (2,), (3,))
PARTS = len(PART_UNITS)
PART_OF = {us[-1]: r for r, us in enumerate(PART_UNITS)}
TILES = [UT * len(us) for us in PART_UNITS]
BLOCKS = [2 * n + NE for n in TILES]
GB = 4
GROUPS = [n // GB for n in BLOCKS]
GROUP0 = [sum(GROUPS[:r]) for r in range(PARTS + 1)]
ALL_GROUPS = GROUP0[PARTS]
EPS = 1e-5
ZEROINGS = 4
LAST_TILES = 4
COMBINES = [n // LAST_TILES for n in TILES]
COMBINE0 = [sum(COMBINES[:r]) for r in range(PARTS + 1)]

Q0, K0, X0, B0, C0, D0, G0, V0, WCOLS = 0, 128, 256, 384, 512, 640, 768, 784, 848
BQ, BK, BX, BB, BC, BD, PRELU, BO, NVEC = 0, 1, 2, 3, 4, 5, 6, 7, 8
RY, RG, RV, NROW = 0, 64, 80, 144
VW, VB, VO, VCOLS = 0, 128, 256, 320


K_TAKE_Y = 0
K_TURN_Y = 1
K_PRELU = 2
K_CENTER = (2, 16)
K_VAR = (4, 17)
K_SCALE = (5, 18)
K_LOW = (5, 19)
K_TURN = (7, 20)
K_PROD = (8, 8, 9, 9, 9, 10, 11, 11)
K_SCAN = (11, 14)
K_OUT = 16
K_RESIDUAL = 16
K_GATE = 22
K_LOGITS = 22
K_CHOOSE = (23, 23, 23)
K_COUNT = (30, 30, 25)
K_PLACE = (31, 31, 24)
K_OWNER = (31, 31, 25)
LEAD = 2
UB = STEPS * BH
MIX_BEATS = UNITS * UB
BEATS = MIX_BEATS + K_OWNER[PARTS - 1] + 1
PROJ_BEAT = 3
HELPED = 3
W12_HIGH_BEATS = [36, 38, MIX_BEATS + 4, MIX_BEATS + 6]
W12_LOW_BEATS = [MIX_BEATS + 1, MIX_BEATS + 2, MIX_BEATS + 8, MIX_BEATS + 9]
SLOT_BUFS = 4
WARM = 60


def build_layer(nc, xT, dgT, wproj, vecs, rows, wvo, wy, w12, w3, out):
    with ExitStack() as ctx:
        def sb(name, shape, dt=F32):
            return ctx.enter_context(nc.sbuf_tensor(name, shape, dt))

        def sem(name):
            return ctx.enter_context(nc.semaphore(name))

        slots_dram = [nc.dram_tensor(f"slots{r}", [BLOCKS[r] * P, 2 * D], F32).ap() for r in range(PARTS)]
        results_dram = [nc.dram_tensor(f"results{r}", [BLOCKS[r] * P, D], F32).ap() for r in range(PARTS)]

        x_raw = sb("x_raw", [P, NB * T])
        x_parts = sb("x_parts", [P, BH * T], F32R)
        qk = sb("qk", [P, HALVES, 3, BH * T], F32R)
        dg = sb("dg", [P, 2, JT, CW])
        v = sb("v", [P, HALVES, BH, JT, D])
        mixed = sb("mixed", [P, 2, BH, CW])
        ret = sb("ret", [P, CW])
        h = sb("h", [P, HALVES, HT, D])
        centered = sb("centered", [P, 2, UT, D])
        squares = sb("squares", [P, 2, UT, D])
        normed = squares
        prelu_neg = squares[:, 0]
        stats = sb("stats", [P, 2, 5, UT])
        ssm_rows = sb("ssm_rows", [P, UT, 2 * D])
        ffn_rows = sb("ffn_rows", [P, HALVES, HT, 2 * D])
        ssm_in = sb("ssm_in", [P, BH, CW], F32R)
        gate_in = sb("gate_in", [P, BH, CW], F32R)
        keep = sb("keep", [P, 2, CW])
        take = sb("take", [P, 2, CW])
        xb = sb("xb", [P, 2, CW])
        cb = sb("cb", [P, 2, CW])
        drive = take
        state = sb("state", [P, BH, 2, CW])
        read = cb
        w_raw = mixed[:, :, :, :].rearrange("p a b n -> p (a b n)")[:, 0:WCOLS]
        w_hi = sb("w_hi", [P, WCOLS], F32R)
        w_lo = sb("w_lo", [P, WCOLS], F32R)
        gate_w = sb("gate_w", [P, 2 * NE], F32R)
        vec = sb("vec", [P, NVEC])
        neg_bd = sb("neg_bd", [P, 1])
        eps = sb("eps", [P, 1])
        spare = sb("spare", [P, 3 * UNITS])
        row = sb("row", [P, NROW])
        wy_sb = sb("wy_sb", [P, D])
        ident = sb("ident", [P, P])
        before = sb("before", [P, P], BF16)
        ones = sb("ones", [P, P], BF16)
        rank_of = sb("rank_of", [P, NE])
        ones16 = sb("ones16", [P, NE])
        block_no = sb("block_no", [1, BLOCKS[0]])
        iota_i = sb("iota_i", [P, BLOCKS[0]], I32)
        zeros = sb("zeros", [P, 256])
        logits = sb("logits", [P, HT, NE])
        best = sb("best", [P, HALVES, 2, HT])
        top = sb("top", [P, 2, HT, NE])
        scratch = [x_raw[:, k * HT * NE:(k + 1) * HT * NE] for k in range(5)]

        def token_first(k, n):
            return scratch[k][:, 0:n * NE].rearrange("p (i e) -> p i e", e=NE)

        def expert_first(k, n):
            return scratch[k][:, 0:n * NE].rearrange("p (e i) -> p e i", i=n)

        owner = x_raw[0:1, 5 * HT * NE:5 * HT * NE + BLOCKS[0] * NE].rearrange("p (n e) -> p n e", e=NE)
        r_b = sb("r_b", [P, HT])
        chosen = sb("chosen", [P, HT, NE], BF16)
        n_int = sb("n_int", [P, NE], I32)
        n_blocks = sb("n_blocks", [P, NE])
        blocks_to = sb("blocks_to", [P, NE])
        first_slot = sb("first_slot", [P, NE])
        slot_f = sb("slot_f", [P, HT, 2])
        slot_i = sb("slot_i", [P, HALVES, HT, 2], I32)
        owner_f = sb("owner_f", [1, BLOCKS[0]])
        owner_i = sb("owner_i", [1, sum(BLOCKS)], I32)
        diff = sb("diff", [P, HALVES, HT])
        expd = sb("expd", [P, HALVES, HT])
        den = sb("den", [P, HALVES, HT])
        weight = sb("weight", [P, HALVES, HT, 2])
        place = dg[:, :, :, :].rearrange("p a j t -> p (a j t)")
        wide, narrow = 2 * GB * P, 2 * GB * D

        def over_dg(at, size, c):
            return place[:, at:at + size].rearrange("p (s n c) -> p s n c", s=2, c=c)

        silu = over_dg(0, wide, HID)
        act = over_dg(wide, wide, HID)
        act_t = over_dg(2 * wide, wide, P)
        slots = place[:, 3 * wide:5 * wide].rearrange("p (s n c) -> p s n c", s=SLOT_BUFS, c=2 * D)
        res = over_dg(5 * wide, narrow, D)
        w3_sb = place[:, 5 * wide + narrow:5 * wide + narrow + NE * D]
        slots_t = qk[:, 0, 2, 0:wide].rearrange("p (s n c) -> p s n c", s=2, c=P)
        w12_hi = qk[:, 0, 0:2, :].rearrange("p a n -> p (a n)")
        w12_lo = qk[:, 1, 0:2, :].rearrange("p a n -> p (a n)")
        w12_stage = x_raw[:, BH * T:NB * T].rearrange("p (s n) -> p s n", s=2)
        back_v = x_raw[:, :].rearrange("p (h i k d) -> p h i k d", h=HALVES, k=2, d=D)

        wvo_sb = mixed[0:D, 1, 1, 0:VCOLS]
        bb = ssm_rows[:, :, :].rearrange("p i c -> p (i c)").rearrange("p (s n) -> p s n", s=2)

        ring = ctx.enter_context(nc.psum_tensor("ring", [P, 4, CW], F32))
        acc = ctx.enter_context(nc.psum_tensor("acc", [P, CW], F32))
        bank5 = ctx.enter_context(nc.psum_tensor("bank5", [P, CW], F32))
        bank6 = ctx.enter_context(nc.psum_tensor("bank6", [P, CW], F32))
        bank7 = ctx.enter_context(nc.psum_tensor("bank7", [P, CW], F32))

        ld_w, ld_vec, ld_wo, ld_wy, ld_w3 = (sem(f"ld_{n}") for n in ("w", "vec", "wo", "wy", "w3"))
        ld_w12 = [sem(f"ld_w12_{i}") for i in range(4)]
        ld_x = [sem(f"ld_x{i}") for i in range(NB)]
        ld_dg = [sem(f"ld_dg{i}") for i in range(8)]
        zeroed = sem("zeroed")
        consts_pool = sem("consts_pool")
        consts = sem("consts")
        w_split_hi, w_split = sem("w_split_hi"), sem("w_split")
        x_high, x_split = sem("x_high"), sem("x_split")
        proj_done, proj_high, proj_free = sem("proj_done"), sem("proj_high"), sem("proj_free")
        scores_done, mixed_done, pv_done, ret_done = sem("scores_done"), sem("mixed_done"), sem("pv_done"), sem("ret_done")
        gate_w_done = sem("gate_w_done")
        vo_done, bb_done = sem("vo_done"), sem("bb_done")
        y_done, y_read = sem("y_done"), sem("y_read")
        center = [sem("center1"), sem("center2")]
        squared = [sem("squared1"), sem("squared2")]
        var_done = [sem("var1"), sem("var2")]
        std_done = [sem("std1"), sem("std2")]
        norm_done = [sem("norm1"), sem("norm2")]
        high_done = [sem("high1"), sem("high2")]
        rows_done = [sem("rows1"), sem("rows2")]
        turned = [sem("turned1"), sem("turned2")]
        in_done = [sem("in1"), sem("in2")]
        d_done, b_done, x_done, c_done = sem("d_done"), sem("b_done"), sem("x_done"), sem("c_done")
        sig_done, bx_done = sem("sig_done"), sem("bx_done")
        xb_done, cb_done = sem("xb_done"), sem("cb_done")
        u_done, scan_done, read_done = sem("u_done"), sem("scan_done"), sem("read_done")
        by_done, wy_done, h2_done = sem("by_done"), sem("wy_done"), sem("h2_done")
        gate_done, logits_done = sem("gate_done"), sem("logits_done")
        chosen_done, count_done, count_read = sem("chosen_done"), sem("count_done"), sem("count_read")
        slot_done, owner_done, diff_done, exp_done = sem("slot_done"), sem("owner_done"), sem("diff_done"), sem("exp_done")
        w12_hi_done, w12_lo_done = sem("w12_hi_done"), sem("w12_lo_done")
        scattered = [sem(f"scattered{i}") for i in range(PARTS)]
        ld_slots = [sem(f"ld_slots{i}") for i in range(SLOT_BUFS)]
        sturned, sin_done = sem("sturned"), sem("sin_done")
        hid_done, silu_done, act_done = sem("hid_done"), sem("silu_done"), sem("act_done")
        aturned, ain_done = sem("aturned"), sem("ain_done")
        res_done, res_read = sem("res_done"), sem("res_read")
        stored = [sem("stored0"), sem("stored1")]
        gathered = [sem(f"gathered{i}") for i in range(COMBINE0[PARTS])]
        combined = sem("combined")
        out_done = sem("out_done")
        dve_step = sem("dve_step")

        block = ctx.enter_context(nc.Block())

        def unit_of(u):
            return u // 2, u % 2

        def part_of_group(n):
            r = max(r for r in range(PARTS) if GROUP0[r] <= n)
            return r, n - GROUP0[r]

        def tiles_of(r):
            hh, c = unit_of(PART_UNITS[r][0])
            return hh, slice(c * UT, c * UT + TILES[r])

        def load_of_dg(th, j):
            return ld_dg[4 * th + j // 2]

        def proj_bank(hh, use):
            return ring[:, use % 4, :] if hh == 0 else (bank5, bank6, bank7)[use % 3][:, :]

        def ssm_bank(n):
            return (bank5, bank6, bank7)[n % 3][:, :]

        def unit_h(u):
            hh, c = unit_of(u)
            return h[:, hh, c * UT:(c + 1) * UT, :]

        def rows_of(which, u):
            hh, c = unit_of(u)
            return ssm_rows[:, :, :] if which == 0 else ffn_rows[:, hh, c * UT:(c + 1) * UT, :]

        def row_of(c0, n, shape):
            return row[:, c0:c0 + n].unsqueeze(1).broadcast_to(shape)

        def add_by(eng, u):
            eng.wait_ge(center[0], u + 1)
            if u >= 1:
                eng.wait_ge(by_done, u)
            eng.tensor_tensor(unit_h(u), unit_h(u), row_of(RY, D, [P, UT, D]), ALU.add).then_inc(by_done, 1)

        def norm_low(eng, which, u):
            eng.wait_ge(high_done[which], u + 1)
            if u >= 1:
                eng.wait_ge(rows_done[which], u)
            eng.tensor_tensor(rows_of(which, u)[:, :, D:2 * D], normed[:, which], rows_of(which, u)[:, :, 0:D],
                              ALU.subtract).then_inc(rows_done[which], 1)

        def ssm_bx(eng, u, b):
            w = 2 * u + b
            eng.wait_ge(bb_done, w + 1)
            eng.wait_ge(xb_done, w + 1)
            if w >= 1:
                eng.wait_ge(bx_done, w)
            eng.tensor_tensor(xb[:, w % 2, :], bb[:, b, :], xb[:, w % 2, :], ALU.mult).then_inc(bx_done, 1)

        def ssm_read(eng, u, b):
            w = 2 * u + b
            eng.wait_ge(scan_done, w + 1)
            eng.wait_ge(cb_done, w + 1)
            if w >= 1:
                eng.wait_ge(read_done, w)
            eng.tensor_tensor(read[:, b, :], state[:, b, u % 2, :], cb[:, w % 2, :], ALU.mult).then_inc(read_done, 1)

        @block.sync
        def _(sp):
            sp.dma_start(w_raw[:, 0:V0], wproj).then_inc(ld_w, 16)
            sp.dma_start(wvo_sb, wvo).then_inc(ld_wo, 16)

            def load_x(b):
                for r in (0, D):
                    sp.dma_start(x_raw[r:r + D, b * T:(b + 1) * T], xT[b]).then_inc(ld_x[b], 16)

            load_x(0)
            sp.dma_start(vec[:, :], vecs).then_inc(ld_vec, 16)
            sp.dma_start(row[:, 0:RV], rows).then_inc(ld_vec, 16)
            load_x(1)
            for th in range(2):
                for jj in range(4):
                    sp.dma_start(dg[:, th, 2 * jj:2 * jj + 2, :],
                                 dgT[2 * jj * P:(2 * jj + 2) * P, th * CW:(th + 1) * CW]
                                 .rearrange("(a p) t -> p a t", p=P)).then_inc(ld_dg[4 * th + jj], 16)
                if th == 0:
                    sp.dma_start(wy_sb[:, :], wy).then_inc(ld_wy, 16)
                    load_x(2)
                    load_x(3)
            sp.wait_ge(consts, 1)
            for r in range(PARTS):
                flat = slots_dram[r].rearrange("(p a z c) e -> p a z (c e)", p=P, a=ZEROINGS, c=2)
                for i in range(ZEROINGS):
                    sp.dma_start(flat[:, i], zeros[:, :].unsqueeze(1).broadcast_to([P, flat.shape[2], 256])).then_inc(zeroed, 16)
            sp.wait_ge(x_split, NB)
            for i in range(4):
                if i >= 2:
                    sp.wait_ge(w12_lo_done, i - 1)
                for r in (0, D):
                    sp.dma_start(w12_stage[r:r + D, i % 2, :], w12[:, i * 1024:(i + 1) * 1024]).then_inc(ld_w12[i], 16)

            sp.wait_ge(mixed_done, MIX_BEATS)
            sp.dma_start(w3_sb[:, :], w3).then_inc(ld_w3, 16)

            def load_slots(n):
                r, g = part_of_group(n)
                if g == 0:
                    sp.wait_ge(scattered[r], 16 * 2 * TILES[r])
                if n >= SLOT_BUFS:
                    sp.wait_ge(sturned, n - SLOT_BUFS + 1)
                sp.dma_start(slots[:, n % SLOT_BUFS, :, :],
                             slots_dram[r][g * GB * P:(g + 1) * GB * P, :]
                             .rearrange("(n p) c -> p n c", p=P)).then_inc(ld_slots[n % SLOT_BUFS], 16)

            def store_results(n):
                r, g = part_of_group(n)
                sp.wait_ge(res_read, n + 1)
                sp.dma_start(results_dram[r][g * GB * P:(g + 1) * GB * P, :]
                             .rearrange("(n p) d -> p n d", p=P), res[:, n % 2]).then_inc(stored[n % 2], 16)

            for n in range(ALL_GROUPS + SLOT_BUFS):
                if n < ALL_GROUPS:
                    load_slots(n)
                if n >= SLOT_BUFS:
                    store_results(n - SLOT_BUFS)

            for r in range(PARTS):
                hh, tiles = tiles_of(r)
                for m in range(COMBINES[r]):
                    sp.wait_ge(combined, COMBINE0[r] + m + 1)
                    t0 = (tiles.start + m * LAST_TILES) // BH
                    nt = LAST_TILES // BH
                    for b in range(BH):
                        sp.dma_start(
                            out[hh * BH + b, t0 * P:(t0 + nt) * P, :].rearrange("(t p) d -> p t d", p=P),
                            h[:, hh, :, :].rearrange("p (t b) d -> p t b d", b=BH)[:, t0:t0 + nt, b, :]
                        ).then_inc(out_done, 16)
            sp.wait_ge(out_done, 16 * COMBINE0[PARTS] * BH)

        @block.gpsimd
        def _(pool):
            n = [0]

            def link(ins):
                n[0] += 1
                ins.then_inc(consts_pool, 1)
                pool.wait_ge(consts_pool, n[0])

            link(pool.memset(ones[:, :], 1.0))
            link(pool.memset(zeros[:, :], 0.0))
            link(pool.memset(ident[:, :], 0.0))
            link(pool.affine_select(out=ident[:, :], in_=ident[:, :], compare_op=ALU.not_equal, fill=1.0,
                                    base=0, pattern=[[-1, P]], channel_multiplier=1))
            link(pool.affine_select(out=before[:, :], in_=ones[:, :], compare_op=ALU.is_gt, fill=0.0,
                                    base=0, pattern=[[1, P]], channel_multiplier=-1))
            link(pool.memset(eps[:, :], EPS))
            link(pool.memset(ones16[:, :], 1.0))
            link(pool.iota(iota_i[:, 0:NE], [[-1, NE]], NE, 0))
            link(pool.tensor_copy(rank_of[:, :], iota_i[:, 0:NE]))
            link(pool.iota(iota_i[:, :], [[1, BLOCKS[0]]], 0, 0))
            pool.tensor_copy(block_no[:, :], iota_i[0:1, :]).then_inc(consts, 1)

            for b in range(BH, NB):
                pool.wait_ge(x_high, b + 1)
                pool.wait_ge(x_split, b)
                c = slice(b % BH * T, (b % BH + 1) * T)
                pool.tensor_tensor(x_parts[D:P, c], x_raw[D:P, b * T:(b + 1) * T], x_parts[D:P, c],
                                   ALU.subtract).then_inc(x_split, 1)

            for m in range(BEATS):
                for u in range(HELPED):
                    k = m - (u + 1) * UB
                    if k == K_CENTER[0] + 1:
                        add_by(pool, u)
                    for b in range(BH):
                        if k == K_PROD[4 * b + 2]:
                            ssm_bx(pool, u, b)
                    if k == K_SCAN[0]:
                        ssm_read(pool, u, 0)
                    for which in range(2):
                        if k == K_SCALE[which]:
                            norm_low(pool, which, u)

            def scatter(r):
                hh, tiles = tiles_of(r)
                pool.wait_ge(zeroed, 16 * PARTS * ZEROINGS)
                pool.wait_ge(rows_done[1], PART_UNITS[r][-1] + 1)
                pool.wait_ge(slot_done, r + 1)
                for i in range(tiles.start, tiles.stop):
                    for k in range(2):
                        pool.indirect_dma_start(
                            out=slots_dram[r], out_offset=bass.IndirectOffsetOnAxis(ap=slot_i[:, hh, i, k:k + 1], axis=0),
                            in_=ffn_rows[:, hh, i, :], in_offset=None).then_inc(scattered[r], 16)

            def gather(r):
                hh, tiles = tiles_of(r)
                for s in range(2):
                    pool.wait_ge(stored[s], 16 * (GROUP0[r + 1] // 2))
                if r == 0:
                    pool.wait_ge(w12_lo_done, 4)
                    pool.wait_ge(owner_done, PARTS)
                for i in range(tiles.start, tiles.stop):
                    for k in range(2):
                        pool.indirect_dma_start(
                            out=back_v[:, hh, i, k, :], out_offset=None, in_=results_dram[r],
                            in_offset=bass.IndirectOffsetOnAxis(ap=slot_i[:, hh, i, k:k + 1], axis=0)
                        ).then_inc(gathered[COMBINE0[r] + (i - tiles.start) // LAST_TILES], 16)

            for r in range(PARTS):
                scatter(r)
            for r in range(PARTS):
                gather(r)

        @block.scalar
        def _(s):
            def projections(hh, uses):
                for use in uses:
                    b, kind, th = (use - 2) // 4, (use - 2) % 4 // 2, use % 2
                    s.wait_ge(proj_done, 10 * hh + use + 1)
                    dst = qk[:, hh, 1 if kind == 0 else 0, b * T + th * CW:b * T + (th + 1) * CW]
                    s.activation(dst, proj_bank(hh, use), ACT.Identity,
                                 bias=vec[:, (BK if kind == 0 else BQ):(BK if kind == 0 else BQ) + 1]).then_inc(proj_high, 1)

            def norm_squares(which, u):
                s.wait_ge(center[which], u + 1)
                if u >= 1:
                    s.wait_ge(rows_done[which], u)
                s.activation(squares[:, which], centered[:, which], ACT.Square).then_inc(squared[which], 1)

            def norm_std(which, u):
                s.wait_ge(var_done[which], u + 1)
                s.activation(stats[:, which, 3, :], stats[:, which, 2, :], ACT.Sqrt, scale=1.0 / D,
                             bias=eps[:, 0:1]).then_inc(std_done[which], 1)

            def norm_high(which, u):
                s.wait_ge(norm_done[which], u + 1)
                if which == 0 and u >= 1:
                    s.wait_ge(turned[0], 2 * u)
                    s.wait_ge(bx_done, 2 * u)
                s.activation(rows_of(which, u)[:, :, 0:D].bitcast(F32R), normed[:, which], ACT.Copy).then_inc(high_done[which], 1)

            def take_turned(which, u):
                dst = ssm_in if which == 0 else gate_in
                for b in range(BH):
                    s.wait_ge(turned[which], 2 * u + b + 1)
                    if u >= 1:
                        if which == 0:
                            s.wait_ge(c_done, 2 * u)
                        else:
                            s.wait_ge(gate_done, u)
                    s.activation(dst[:, b, :], (bank6, bank7)[b][:, :], ACT.Copy).then_inc(in_done[which], 1)

            def take_product(u, n):
                b, kind = divmod(n, 4)
                w = 2 * u + b
                bank = ssm_bank(n)
                s.wait_ge((d_done, b_done, x_done, c_done)[kind], w + 1)
                if kind == 0:
                    if w >= 2:
                        s.wait_ge(scan_done, w - 1)
                    s.activation(take[:, w % 2, :], bank, ACT.Sigmoid, bias=vec[:, BD:BD + 1]).then_inc(sig_done, 1)
                    s.activation(keep[:, w % 2, :], bank, ACT.Sigmoid, scale=-1.0, bias=neg_bd[:, 0:1]).then_inc(sig_done, 1)
                elif kind == 1:
                    s.wait_ge(turned[0], 2 * u + 2)
                    s.activation(bb[:, b, :], bank, ACT.Identity, bias=vec[:, BB:BB + 1]).then_inc(bb_done, 1)
                elif kind == 2:
                    if w >= 2:
                        s.wait_ge(u_done, w - 1)
                    s.activation(xb[:, w % 2, :], bank, ACT.Identity, bias=vec[:, BX:BX + 1]).then_inc(xb_done, 1)
                else:
                    if u >= 1:
                        s.wait_ge(wy_done, u)
                    s.activation(cb[:, w % 2, :], bank, ACT.Identity, bias=vec[:, BC:BC + 1]).then_inc(cb_done, 1)

            s.wait_ge(ld_w, 16)
            s.activation(w_hi[:, 0:V0], w_raw[:, 0:V0], ACT.Copy).then_inc(w_split_hi, 1)
            s.wait_ge(w_split, 1)
            s.activation(gate_w[:, 0:NE], w_hi[:, G0:G0 + NE].bitcast(F32), ACT.Copy)
            s.activation(gate_w[:, NE:2 * NE], w_lo[:, G0:G0 + NE].bitcast(F32), ACT.Copy).then_inc(gate_w_done, 1)
            s.wait_ge(vo_done, 1)
            s.activation(w_hi[:, V0:V0 + D], acc[:, 0:D], ACT.Copy).then_inc(w_split_hi, 1)

            def x_highs(hh):
                for b in range(hh * BH, (hh + 1) * BH):
                    s.wait_ge(ld_x[b], 32)
                    if b == BH:
                        s.wait_ge(proj_done, 10)
                    c = b % BH * T
                    s.activation(x_parts[:, c:c + T], x_raw[:, b * T:(b + 1) * T], ACT.Copy).then_inc(x_high, 1)

            x_highs(0)
            s.wait_ge(ld_vec, 32)
            projections(0, range(2, 10))
            s.wait_ge(consts, 1)
            x_highs(1)

            def take_y(u):
                s.wait_ge(pv_done, (u + 1) * STEPS)
                if u >= 1:
                    s.wait_ge(y_done, u)
                s.activation(ret[:, :], acc[:, :], ACT.Identity, bias=vec[:, BO:BO + 1]).then_inc(ret_done, 1)

            def w12_high(i):
                s.wait_ge(ld_w12[i], 32)
                s.wait_ge(scores_done, 2 * UB)
                c = slice(i * 1024, (i + 1) * 1024)
                s.activation(w12_hi[:, c], w12_stage[:, i % 2, :], ACT.Copy).then_inc(w12_hi_done, 1)

            for m in range(BEATS):
                if m - PROJ_BEAT in range(2, 10):
                    projections(1, [m - PROJ_BEAT])
                for u in range(UNITS):
                    k = m - (u + 1) * UB
                    if k == K_TAKE_Y:
                        take_y(u)
                    if k == K_SCALE[0] + 1:
                        s.activation(spare[:, 3 * u:3 * u + 1], eps[:, :], ACT.Sigmoid)
                    for which in range(2):
                        if k == K_CENTER[which] - 1:
                            s.activation(spare[:, 3 * u + 1 + which:3 * u + 2 + which], eps[:, :], ACT.Sqrt)
                        if k == K_CENTER[which]:
                            norm_squares(which, u)
                        if k == K_VAR[which]:
                            norm_std(which, u)
                        if k == K_SCALE[which]:
                            norm_high(which, u)
                        if k == K_TURN[which]:
                            take_turned(which, u)
                    for n in range(4 * BH):
                        if k == K_PROD[n]:
                            take_product(u, n)
                    if u in PART_OF and k == K_PLACE[PART_OF[u]]:
                        r = PART_OF[u]
                        hh, tiles = tiles_of(r)
                        s.wait_ge(diff_done, r + 1)
                        s.activation(expd[:, hh, tiles], diff[:, hh, tiles], ACT.Exp).then_inc(exp_done, 1)
                if m in W12_HIGH_BEATS:
                    w12_high(W12_HIGH_BEATS.index(m))

            def take_slots(n):
                s.wait_ge(sturned, n + 1)
                if n >= 2:
                    s.wait_ge(hid_done, n - 1)
                s.activation(slots_t[:, n % 2].rearrange("p n c -> p (n c)"), ring[:, 0, :], ACT.Copy).then_inc(sin_done, 1)

            def silus(n):
                s.wait_ge(hid_done, n + 1)
                if n >= 2:
                    s.wait_ge(act_done, n - 1)
                h1 = ring[:, 1:3, :].rearrange("p a (n c) -> p (a n) c", c=2 * HID)[:, :, 0:HID]
                s.activation(silu[:, n % 2], h1, ACT.Silu).then_inc(silu_done, 1)

            def take_act(n):
                s.wait_ge(aturned, n + 1)
                if n >= 2:
                    s.wait_ge(res_done, n - 1)
                s.activation(act_t[:, n % 2].rearrange("p n c -> p (n c)"), ring[:, 3, :], ACT.Copy).then_inc(ain_done, 1)

            for n in range(ALL_GROUPS + 2):
                if n < ALL_GROUPS:
                    take_slots(n)
                if 1 <= n <= ALL_GROUPS:
                    silus(n - 1)
                if n >= 2:
                    take_act(n - 2)

        @block.tensor
        def _(pe):
            def split_product(dst, moving, lo_col, n, last=True):
                pe.matmul(dst, w_hi[:, lo_col:lo_col + n], moving, start=True, stop=False)
                return pe.matmul(dst, w_lo[:, lo_col:lo_col + n], moving, start=False, stop=True)

            def projections(hh, uses):
                for use in uses:
                    banks = 3 if hh else 4
                    if use >= banks:
                        pe.wait_ge(proj_free, 10 * hh + use - banks + 1)
                    if use < 2:
                        b = use
                        pe.wait_ge(x_split, hh * BH + b + 1)
                        for j in range(JT):
                            x0 = b * T + j * P
                            for part, w in enumerate((w_hi, w_lo)):
                                mm = pe.matmul(proj_bank(hh, use)[:, j * D:(j + 1) * D], x_parts[:, x0:x0 + P],
                                               w[:, V0:V0 + D], start=part == 0, stop=part == 1)
                    else:
                        b, kind, th = (use - 2) // 4, (use - 2) % 4 // 2, use % 2
                        x0 = b * T + th * CW
                        mm = split_product(proj_bank(hh, use), x_parts[:, x0:x0 + CW], K0 if kind == 0 else Q0, P)
                    mm.then_inc(proj_done, 1)

            def scores(m):
                u, j, b = m // UB, m % UB // BH, m % BH
                hh, th = unit_of(u)
                if m % UB == 0:
                    pe.wait_ge(proj_free, 10 * hh + 10)
                if m >= 4:
                    pe.wait_ge(mixed_done, m - 3)
                for part in range(2):
                    mm = pe.matmul(ring[:, m % 4, :], qk[:, hh, 1 + part, b * T + j * P:b * T + (j + 1) * P],
                                   qk[:, hh, 0, b * T + th * CW:b * T + (th + 1) * CW],
                                   start=part == 0, stop=part == 1)
                mm.then_inc(scores_done, 1)

            def pv(step):
                u, j = step // STEPS, step % STEPS
                pe.wait_ge(mixed_done, BH * (step + 1))
                if j == 0 and u >= 1:
                    pe.wait_ge(ret_done, u)
                for b in range(BH):
                    mm = pe.matmul(acc[b * D:(b + 1) * D, :], v[:, u // 2, b, j, :], mixed[:, step % 2, b, :],
                                   start=j == 0, stop=j == JT - 1)
                mm.then_inc(pv_done, 1)

            def turn_y(u):
                pe.wait_ge(ret_done, u + 1)
                if u == 0:
                    pe.wait_ge(proj_free, 20)
                else:
                    pe.wait_ge(h2_done, u)
                for t in range(UT // BH):
                    mm = pe.transpose(bank5[:, t * P:(t + 1) * P], ret[:, t * P:(t + 1) * P], ident[:, :])
                mm.then_inc(y_done, 1)

            def turn_rows(which, u):
                rows_ = rows_of(which, u)
                pe.wait_ge(rows_done[which], u + 1)
                if which == 1:
                    pe.wait_ge(bb_done, 2 * u + 2)
                    pe.wait_ge(cb_done, 2 * u + 2)
                elif u == 0:
                    pe.wait_ge(proj_free, 20)
                else:
                    pe.wait_ge(in_done[1], 2 * u)
                    pe.wait_ge(logits_done, u)
                for b in range(BH):
                    for t in range(UT // BH):
                        mm = pe.transpose((bank6, bank7)[b][:, t * P:(t + 1) * P], rows_[:, t * BH + b, :], ident[:, :])
                    mm.then_inc(turned[which], 1)

            def product(u, n):
                b, kind = divmod(n, 4)
                w = 2 * u
                pe.wait_ge(in_done[0], w + b + 1)
                before_ = ((y_read, u + 1), (in_done[0], w + 1), (in_done[0], w + 2), (sig_done, 2 * w + 2),
                           (bb_done, w + 1), (xb_done, w + 1), (cb_done, w + 1), (sig_done, 2 * w + 4))[n]
                pe.wait_ge(*before_)
                split_product(ssm_bank(n), ssm_in[:, b, :], (D0, B0, X0, C0)[kind], CH
                              ).then_inc((d_done, b_done, x_done, c_done)[kind], 1)

            def ssm_out(u):
                if u == 0:
                    pe.wait_ge(ld_wy, 16)
                pe.wait_ge(xb_done, 2 * u + 2)
                if u >= 2:
                    pe.wait_ge(count_read, u - 1)
                pe.wait_ge(read_done, 2 * u + 2)
                for i in range(UT):
                    b, t = i % BH, i // BH
                    mm = pe.matmul(bank5[:, i * D:(i + 1) * D], read[:, b, t * P:(t + 1) * P], wy_sb[:, :],
                                   start=True, stop=True)
                mm.then_inc(wy_done, 1)

            def gate(u):
                pe.wait_ge(gate_w_done, 1)
                pe.wait_ge(in_done[1], 2 * u + 2)
                for i in range(UT):
                    b, t = i % BH, i // BH
                    mm = pe.matmul(bank6[:, i * 2 * NE:(i + 1) * 2 * NE], gate_in[:, b, t * P:(t + 1) * P],
                                   gate_w[:, :], start=True, stop=True)
                mm.then_inc(gate_done, 1)

            def count(r):
                _, tiles = tiles_of(r)
                n = TILES[r] * NE
                pe.wait_ge(chosen_done, r + 1)
                if r < PARTS - 1:
                    pe.wait_ge(xb_done, 2 * (PART_UNITS[r][-1] + 2))
                else:
                    pe.wait_ge(h2_done, UNITS)
                picked = chosen[:, tiles, :].rearrange("p i e -> p (i e)")
                pe.matmul(bank5[:, 0:n], before[:, :], picked, start=True, stop=True)
                pe.matmul(bank5[:, n:2 * n], ones[:, :], picked, start=True, stop=True).then_inc(count_done, 1)

            pe.wait_ge(consts_pool, 1)
            for i in range(WARM):
                pe.matmul(ring[:, 0, 0:P], ones[:, :], ones[:, :], start=True, stop=True)
            pe.wait_ge(ld_wo, 16)
            pe.matmul(acc[:, 0:D], wvo_sb[:, VW:VW + P], wvo_sb[:, VO:VO + D], start=True, stop=True)
            pe.matmul(acc[:, D:2 * D], wvo_sb[:, VB:VB + P], wvo_sb[:, VO:VO + D], start=True, stop=True).then_inc(vo_done, 1)
            pe.wait_ge(w_split, 2)
            projections(0, range(10))
            pe.wait_ge(consts, 1)
            for m in range(LEAD):
                scores(m)
            for m in range(BEATS):
                if m + LEAD < MIX_BEATS:
                    scores(m + LEAD)
                if m % BH == 1 and BH < m <= MIX_BEATS + 1:
                    pv(m // BH - 1)
                if m - PROJ_BEAT in range(10):
                    projections(1, [m - PROJ_BEAT])
                for u in range(UNITS):
                    k = m - (u + 1) * UB
                    if k == K_TURN_Y:
                        turn_y(u)
                    if k == K_TURN[0]:
                        turn_rows(0, u)
                    for n in range(4 * BH):
                        if k == K_PROD[n]:
                            product(u, n)
                    if k == K_OUT:
                        ssm_out(u)
                    if k == K_TURN[1]:
                        turn_rows(1, u)
                    if k == K_GATE:
                        gate(u)
                    if u in PART_OF and k == K_COUNT[PART_OF[u]]:
                        count(PART_OF[u])

            experts = {}

            def turn_slots(n):
                pe.wait_ge(ld_slots[n % SLOT_BUFS], 16 * (n // SLOT_BUFS + 1))
                if n >= 1:
                    pe.wait_ge(sin_done, n)
                for k in range(GB):
                    mm = pe.transpose(ring[:, 0, k * P:(k + 1) * P], slots[:, n % SLOT_BUFS, k, :], ident[:, :])
                mm.then_inc(sturned, 1)

            def hidden(n):
                r, g = part_of_group(n)
                if g == 0:
                    pe.wait_ge(owner_done, r + 1)
                if n == 0:
                    pe.wait_ge(w12_lo_done, 4)
                _, experts[n] = nc.values_load_multi_w_load_instructions(
                    owner_i[0:1, n * GB:(n + 1) * GB], engines=[PE_ENGINE], min_val=0, max_val=NE - 1,
                    skip_runtime_bounds_check_because="the owner of a block is at most NE - 1")
                pe.wait_ge(sin_done, n + 1)
                if n >= 1:
                    pe.wait_ge(act_done, n)
                for k in range(GB):
                    for part, w in enumerate((w12_hi, w12_lo)):
                        mm = pe.matmul(ring[:, 1 + k // 2, k % 2 * 2 * HID:(k % 2 + 1) * 2 * HID], slots_t[:, n % 2, k, :],
                                       w[:, bass.ds(experts[n][k] * (2 * HID), 2 * HID)], start=part == 0, stop=part == 1)
                mm.then_inc(hid_done, 1)

            def turn_act(n):
                pe.wait_ge(act_done, n + 1)
                if n >= 1:
                    pe.wait_ge(ain_done, n)
                for k in range(GB):
                    mm = pe.transpose(ring[:, 3, k * P:(k + 1) * P], act[:, n % 2, k, :], ident[:, :])
                mm.then_inc(aturned, 1)

            def result(n):
                if n == 0:
                    pe.wait_ge(ld_w3, 16)
                    pe.wait_ge(ret_done, UNITS)
                else:
                    pe.wait_ge(res_read, n)
                pe.wait_ge(ain_done, n + 1)
                for k in range(GB):
                    mm = pe.matmul(acc[:, k * D:(k + 1) * D], act_t[:, n % 2, k, :],
                                   w3_sb[:, bass.ds(experts[n][k] * D, D)], start=True, stop=True)
                mm.then_inc(res_done, 1)

            pe.wait_ge(mixed_done, MIX_BEATS)
            for n in range(ALL_GROUPS + 3):
                if n < ALL_GROUPS:
                    turn_slots(n)
                if 1 <= n <= ALL_GROUPS:
                    hidden(n - 1)
                if 2 <= n <= ALL_GROUPS + 1:
                    turn_act(n - 2)
                if n >= 3:
                    result(n - 3)

        @block.vector
        def _(dve):
            steps = [0]

            def link(ins):
                steps[0] += 1
                ins.then_inc(dve_step, 1)
                dve.wait_ge(dve_step, steps[0])

            def x_lows():
                for b in range(BH):
                    dve.wait_ge(x_high, b + 1)
                    c = slice(b % BH * T, (b % BH + 1) * T)
                    dve.tensor_tensor(x_parts[D:P, c], x_raw[D:P, b * T:(b + 1) * T], x_parts[D:P, c],
                                      ALU.subtract).then_inc(x_split, 1)

            def projections(hh, uses):
                for use in uses:
                    if use < 2:
                        dve.wait_ge(proj_done, 10 * hh + use + 1)
                        dve.tensor_tensor(v[:, hh, use], proj_bank(hh, use).rearrange("p (j d) -> p j d", d=D),
                                          row_of(RV, D, [P, JT, D]), ALU.add).then_inc(proj_free, 1)
                        continue
                    b, kind, th = (use - 2) // 4, (use - 2) % 4 // 2, use % 2
                    c = slice(b * T + th * CW, b * T + (th + 1) * CW)
                    dve.wait_ge(proj_high, 8 * hh + use - 1)
                    r = slice(0, P) if kind == 0 else slice(D, P)
                    dve.scalar_tensor_tensor(out=qk[r, hh, 2 if kind == 0 else 0, c], in0=proj_bank(hh, use)[r, :],
                                             scalar=vec[r, (BK if kind == 0 else BQ):(BK if kind == 0 else BQ) + 1],
                                             in1=qk[r, hh, 1 if kind == 0 else 0, c], op0=ALU.add, op1=ALU.subtract
                                             ).then_inc(proj_free, 1)

            def mix_beat(m):
                u, j, b = m // UB, m % UB // BH, m % BH
                if u < 2 and j % 2 == 0 and b == 0:
                    dve.wait_ge(load_of_dg(u, j), 16)
                dve.wait_ge(scores_done, m + 1)
                if m >= 2 * BH:
                    dve.wait_ge(pv_done, m // BH - 1)
                dve.tensor_tensor(mixed[:, m // BH % 2, b, :], ring[:, m % 4, :], dg[:, u % 2, j, :],
                                  ALU.mult).then_inc(mixed_done, 1)

            def prelu(u):
                dve.wait_ge(y_done, u + 1)
                if u >= 1:
                    dve.wait_ge(rows_done[0], u)
                y = bank5[:, :].rearrange("p (i d) -> p i d", d=D)
                link(dve.tensor_scalar(prelu_neg, y, 0.0, vec[:, PRELU:PRELU + 1], ALU.min, ALU.mult))
                dve.scalar_tensor_tensor(out=unit_h(u), in0=y, scalar=0.0, in1=prelu_neg, op0=ALU.max,
                                         op1=ALU.add).then_inc(y_read, 1)

            def norm_center(which, u):
                hu = unit_h(u)
                dve.wait_ge((y_read, h2_done)[which], u + 1)
                link(dve.tensor_reduce(stats[:, which, 0, :], hu, AX_X, ALU.add))
                link(dve.tensor_scalar(stats[:, which, 1, :], stats[:, which, 0, :], -1.0 / D, None, ALU.mult))
                dve.tensor_tensor(centered[:, which], hu, stats[:, which, 1, :].unsqueeze(2).broadcast_to([P, UT, D]),
                                  ALU.add).then_inc(center[which], 1)

            def norm_var(which, u):
                dve.wait_ge(squared[which], u + 1)
                dve.tensor_reduce(stats[:, which, 2, :], squares[:, which], AX_X, ALU.add).then_inc(var_done[which], 1)

            def norm_scale(which, u):
                dve.wait_ge(std_done[which], u + 1)
                link(dve.reciprocal(stats[:, which, 4, :], stats[:, which, 3, :]))
                if u >= 1:
                    dve.wait_ge(high_done[which], u)
                dve.tensor_tensor(normed[:, which], centered[:, which],
                                  stats[:, which, 4, :].unsqueeze(2).broadcast_to([P, UT, D]), ALU.mult).then_inc(norm_done[which], 1)

            def ssm_scan(u, b):
                w = 2 * u + b
                dve.wait_ge(bx_done, w + 1)
                dve.wait_ge(sig_done, 2 * w + 2)
                dve.tensor_tensor(drive[:, w % 2, :], take[:, w % 2, :], xb[:, w % 2, :], ALU.mult).then_inc(u_done, 1)
                dve.wait_ge(u_done, w + 1)
                if u >= 2:
                    dve.wait_ge(read_done, w - 3)
                start = 0.0 if u % 2 == 0 else state[:, b, 0, CW - 1:CW]
                dve.tensor_tensor_scan(state[:, b, u % 2, :], keep[:, w % 2, :], drive[:, w % 2, :], start,
                                       ALU.mult, ALU.add).then_inc(scan_done, 1)

            def residual(u):
                hu = unit_h(u)
                dve.wait_ge(wy_done, u + 1)
                dve.wait_ge(by_done, u + 1)
                dve.tensor_tensor(hu, bank5[:, :].rearrange("p (i d) -> p i d", d=D), hu, ALU.add).then_inc(h2_done, 1)

            def w12_low(i):
                dve.wait_ge(scores_done, MIX_BEATS)
                dve.wait_ge(w12_hi_done, i + 1)
                c = slice(i * 1024, (i + 1) * 1024)
                dve.tensor_tensor(w12_lo[:, c], w12_stage[:, i % 2, :], w12_hi[:, c], ALU.subtract).then_inc(w12_lo_done, 1)

            def take_logits(u):
                hh, c = unit_of(u)
                dve.wait_ge(gate_done, u + 1)
                parts = bank6[:, 0:2 * UT * NE].rearrange("p (i a e) -> p i a e", a=2, e=NE)
                lg = logits[:, c * UT:(c + 1) * UT, :]
                link(dve.tensor_tensor(lg, parts[:, :, 0, :], row_of(RG, NE, [P, UT, NE]), ALU.add))
                dve.tensor_tensor(lg, parts[:, :, 1, :], lg, ALU.add).then_inc(logits_done, 1)

            def choose(r):
                hh, tiles = tiles_of(r)
                full = [P, TILES[r], NE]
                lg, mark, score = logits[:, tiles, :], token_first(0, TILES[r]), r_b[:, tiles]
                dve.wait_ge(logits_done, PART_UNITS[r][-1] + 1)
                for k in range(2):
                    high = best[:, hh, k, tiles]
                    link(dve.tensor_reduce(high, lg, AX_X, ALU.max))
                    link(dve.tensor_tensor(mark, lg, high.unsqueeze(2).broadcast_to(full), ALU.is_equal))
                    link(dve.tensor_tensor(mark, mark, rank_of[:, :].unsqueeze(1).broadcast_to(full), ALU.mult))
                    link(dve.tensor_reduce(score, mark, AX_X, ALU.max))
                    link(dve.tensor_tensor(top[:, k, tiles], mark, score.unsqueeze(2).broadcast_to(full), ALU.is_equal))
                    if k == 0:
                        link(dve.scalar_tensor_tensor(out=lg, in0=top[:, 0, tiles], scalar=-3e38, in1=lg,
                                                      op0=ALU.mult, op1=ALU.add))
                dve.tensor_tensor(chosen[:, tiles, :], top[:, 0, tiles], top[:, 1, tiles], ALU.add).then_inc(chosen_done, 1)
                dve.tensor_tensor(diff[:, hh, tiles], best[:, hh, 1, tiles], best[:, hh, 0, tiles],
                                  ALU.subtract).then_inc(diff_done, 1)

            def place_tokens(r):
                hh, tiles = tiles_of(r)
                nt = TILES[r]
                slot, found = token_first(1, nt), token_first(0, nt)
                counts, counts_to, not_first = (expert_first(k, nt) for k in (2, 3, 4))
                offset = counts_to
                flat = "p e i -> p (e i)"
                link(dve.memset(not_first, 1.0))
                link(dve.memset(not_first[:, :, 0:1], 0.0))
                dve.wait_ge(count_done, r + 1)
                before_it = bank5[:, 0:nt * NE].rearrange("p (i e) -> p i e", e=NE)
                in_tile = bank5[:, nt * NE:2 * nt * NE].rearrange("p (i e) -> p e i", e=NE)
                link(dve.tensor_copy(counts, in_tile))
                link(dve.tensor_tensor_scan(counts_to.rearrange(flat), not_first.rearrange(flat),
                                            counts.rearrange(flat), 0.0, ALU.mult, ALU.add))
                link(dve.tensor_scalar(n_int[:, :], counts_to[:, :, nt - 1], float(P - 1), None, ALU.add))
                link(dve.tensor_scalar(n_int[:, :], n_int[:, :], 7, None, ALU.logical_shift_right))
                link(dve.tensor_copy(n_blocks[:, :], n_int[:, :]))
                link(dve.tensor_tensor_scan(blocks_to[:, :], ones16[:, :], n_blocks[:, :], 0.0, ALU.mult, ALU.add))
                link(dve.tensor_tensor(first_slot[:, :], blocks_to[:, :], n_blocks[:, :], ALU.subtract))
                link(dve.tensor_tensor(offset, counts_to, counts, ALU.subtract))
                link(dve.scalar_tensor_tensor(out=offset, in0=first_slot[:, :].unsqueeze(2).broadcast_to([P, NE, nt]),
                                              scalar=float(P), in1=offset, op0=ALU.mult, op1=ALU.add))
                dve.tensor_tensor(slot, before_it, offset.rearrange("p e i -> p i e"), ALU.add).then_inc(count_read, 1)
                dve.wait_ge(count_read, r + 1)
                for k in range(2):
                    link(dve.tensor_tensor(found, slot, top[:, k, tiles], ALU.mult))
                    link(dve.tensor_reduce(slot_f[:, tiles, k], found, AX_X, ALU.add))
                dve.tensor_copy(slot_i[:, hh, tiles], slot_f[:, tiles, :]).then_inc(slot_done, 1)

            def owners(r):
                n, at = BLOCKS[r], GROUP0[r] * GB
                link(dve.tensor_tensor(owner[:, 0:n, :], blocks_to[0:1, :].unsqueeze(1).broadcast_to([1, n, NE]),
                                       block_no[:, 0:n].unsqueeze(2).broadcast_to([1, n, NE]), ALU.is_le))
                link(dve.tensor_reduce(owner_f[:, 0:n], owner[:, 0:n, :], AX_X, ALU.add))
                link(dve.tensor_scalar(owner_f[:, 0:n], owner_f[:, 0:n], float(NE - 1), None, ALU.min))
                dve.tensor_copy(owner_i[:, at:at + n], owner_f[:, 0:n]).then_inc(owner_done, 1)

            def weights(r):
                hh, tiles = tiles_of(r)
                dve.wait_ge(exp_done, r + 1)
                link(dve.tensor_scalar(den[:, hh, tiles], expd[:, hh, tiles], 1.0, None, ALU.add))
                link(dve.reciprocal(weight[:, hh, tiles, 0], den[:, hh, tiles]))
                link(dve.tensor_tensor(weight[:, hh, tiles, 1], expd[:, hh, tiles], weight[:, hh, tiles, 0], ALU.mult))

            dve.wait_ge(w_split_hi, 1)
            dve.tensor_tensor(w_lo[:, 0:V0], w_raw[:, 0:V0], w_hi[:, 0:V0], ALU.subtract).then_inc(w_split, 1)
            dve.wait_ge(w_split_hi, 2)
            dve.tensor_tensor(w_lo[:, V0:V0 + D], acc[:, 0:D], w_hi[:, V0:V0 + D], ALU.subtract).then_inc(w_split, 1)
            link(dve.tensor_copy(row[:, RV:RV + D], acc[:, D:2 * D]))
            x_lows()
            dve.wait_ge(ld_vec, 32)
            link(dve.tensor_scalar(neg_bd[:, :], vec[:, BD:BD + 1], -1.0, None, ALU.mult))
            projections(0, range(10))
            dve.wait_ge(consts, 1)
            for m in range(BEATS):
                if m < MIX_BEATS:
                    mix_beat(m)
                if m - PROJ_BEAT in range(2):
                    projections(1, [m - PROJ_BEAT])
                if m - PROJ_BEAT - 1 in range(2, 10):
                    projections(1, [m - PROJ_BEAT - 1])
                for u in range(UNITS):
                    k = m - (u + 1) * UB
                    if k == K_PRELU:
                        prelu(u)
                    if k == K_RESIDUAL:
                        residual(u)
                    for which in range(2):
                        if k == K_CENTER[which]:
                            norm_center(which, u)
                        if k == K_VAR[which]:
                            norm_var(which, u)
                        if k == K_SCALE[which]:
                            norm_scale(which, u)
                        if k == K_LOW[which] and u >= HELPED:
                            norm_low(dve, which, u)
                    if k == K_CENTER[0] + 1 and u >= HELPED:
                        add_by(dve, u)
                    for b in range(BH):
                        if k == K_SCAN[b]:
                            if u >= HELPED:
                                ssm_bx(dve, u, b)
                            ssm_scan(u, b)
                            if u >= HELPED or b == BH - 1:
                                ssm_read(dve, u, b)
                    if k == K_LOGITS:
                        take_logits(u)
                    if u in PART_OF and k == K_CHOOSE[PART_OF[u]]:
                        choose(PART_OF[u])
                    if u in PART_OF and k == K_PLACE[PART_OF[u]]:
                        place_tokens(PART_OF[u])
                    if u in PART_OF and k == K_OWNER[PART_OF[u]]:
                        owners(PART_OF[u])
                if m in W12_LOW_BEATS:
                    w12_low(W12_LOW_BEATS.index(m))
            for r in range(PARTS):
                weights(r)

            def gated(n):
                dve.wait_ge(silu_done, n + 1)
                if n >= 2:
                    dve.wait_ge(aturned, n - 1)
                h2 = ring[:, 1:3, :].rearrange("p a (n c) -> p (a n) c", c=2 * HID)[:, :, HID:2 * HID]
                dve.tensor_tensor(act[:, n % 2], h2, silu[:, n % 2], ALU.mult).then_inc(act_done, 1)

            def take_result(n):
                dve.wait_ge(res_done, n + 1)
                if n >= 2:
                    dve.wait_ge(stored[n % 2], 16 * (n // 2))
                dve.tensor_copy(res[:, n % 2], acc[:, 0:GB * D].rearrange("p (n d) -> p n d", d=D)).then_inc(res_read, 1)

            for n in range(1, ALL_GROUPS + 3):
                if n <= ALL_GROUPS:
                    gated(n - 1)
                if n >= 3:
                    take_result(n - 3)

            for r in range(PARTS):
                hh, tiles = tiles_of(r)
                for m in range(COMBINES[r]):
                    i = slice(tiles.start + m * LAST_TILES, tiles.start + (m + 1) * LAST_TILES)
                    dve.wait_ge(gathered[COMBINE0[r] + m], 16 * 2 * LAST_TILES)
                    got = back_v[:, hh, i]
                    link(dve.tensor_tensor(got, got, weight[:, hh, i, :].unsqueeze(3).broadcast_to([P, LAST_TILES, 2, D]), ALU.mult))
                    link(dve.tensor_tensor(h[:, hh, i], h[:, hh, i], got[:, :, 0, :], ALU.add))
                    dve.tensor_tensor(h[:, hh, i], h[:, hh, i], got[:, :, 1, :], ALU.add).then_inc(combined, 1)


def kernel(**inputs):
    import numpy as np
    import concourse.bacc as bacc
    from concourse.bass_utils import run_bass_kernel_spmd as run

    def a(name):
        return np.asarray(inputs[name])

    def both(m):
        return np.concatenate([m, m], axis=0)

    wq, wk, wbc = a("L0_tok_Wq"), a("L0_tok_Wk"), a("L0_attn_Wbc")
    n = wbc.shape[1] // 2
    bbc = a("L0_attn_bbc")
    wproj = both(np.concatenate([wq, wq, wk, wk, a("L0_attn_Wx"), wbc[:, :n], wbc[:, n:],
                                 a("L0_attn_Wd"), a("L0_ffn_gate_w")], axis=1))
    vecs = np.stack([both(a("L0_tok_bq")), both(a("L0_tok_bk")), a("L0_attn_bx"), bbc[:n], bbc[n:], a("L0_attn_bd"),
                     np.broadcast_to(a("L0_tok_prelu_a"), (P,)), both(a("L0_tok_bo"))], axis=1)
    rows = np.broadcast_to(np.concatenate([a("L0_attn_by"), a("L0_ffn_gate_b")]), (P, RV))
    wv_t = a("L0_tok_Wv").T
    wvo = np.concatenate([wv_t, wv_t, np.broadcast_to(a("L0_tok_bv")[:, None], (D, P)), a("L0_tok_Wo")], axis=1)
    w12 = np.concatenate([a("L0_ffn_w1"), a("L0_ffn_w2")], axis=2).transpose(1, 0, 2).reshape(D, -1)
    arrays = {
        "xT": a("x").reshape(NB, T, D).transpose(0, 2, 1),
        "dgT": a("L0_tok_d_gamma_batched").T,
        "wproj": wproj, "vecs": vecs, "rows": rows,
        "wvo": wvo, "wy": a("L0_attn_Wy"), "w12": w12,
        "w3": a("L0_ffn_w3").transpose(1, 0, 2).reshape(HID, -1),
    }
    arrays = {k: np.ascontiguousarray(m) for k, m in arrays.items()}
    nc = bacc.Bacc("TRN2", target_bir_lowering=False, num_devices=1)
    args = [nc.dram_tensor(k, m.shape, mybir.dt.from_np(m.dtype), kind="ExternalInput").ap() for k, m in arrays.items()]
    out = nc.dram_tensor("out", (NB, T, D), F32, kind="ExternalOutput").ap()
    build_layer(nc, *args, out)
    r = run(nc, [arrays], core_ids=[0])
    return r.results[0]["out"]
```

```python
from contextlib import ExitStack

import concourse.bass as bass
from concourse import mybir

F32 = mybir.dt.float32
F32R = mybir.dt.float32r
BF16 = mybir.dt.bfloat16
I32 = mybir.dt.int32
ALU = mybir.AluOpType
ACT = mybir.ActivationFunctionType
AX_X = mybir.AxisListType.X
PE_ENGINE = mybir.EngineType.PE

P = 128
NB, T, D = 4, 1024, 64
CH = 128
NE, HID = 16, 128
HALVES, UNITS = 2, 4
BH = NB // HALVES
CW = T // 2
JT = T // P
UT = BH * CW // P
HT = 2 * UT
STEPS = JT
PART_UNITS = ((0, 1), (2,), (3,))
PARTS = len(PART_UNITS)
PART_OF = {us[-1]: r for r, us in enumerate(PART_UNITS)}
TILES = [UT * len(us) for us in PART_UNITS]
BLOCKS = [2 * n + NE for n in TILES]
GB = 4
GROUPS = [n // GB for n in BLOCKS]
GROUP0 = [sum(GROUPS[:r]) for r in range(PARTS + 1)]
ALL_GROUPS = GROUP0[PARTS]
EPS = 1e-5
ZEROINGS = 4
LAST_TILES = 4
COMBINES = [n // LAST_TILES for n in TILES]
COMBINE0 = [sum(COMBINES[:r]) for r in range(PARTS + 1)]

Q0, K0, X0, B0, C0, D0, G0, V0, WCOLS = 0, 128, 256, 384, 512, 640, 768, 784, 848
BQ, BK, BX, BB, BC, BD, PRELU, BO, NVEC = 0, 1, 2, 3, 4, 5, 6, 7, 8
RY, RG, RV, NROW = 0, 64, 80, 144
VW, VB, VO, VCOLS = 0, 128, 256, 320


K_TAKE_Y = 0
K_TURN_Y = 2
K_PRELU = (2, 2)
K_CENTER = ((3, 3), (16, 17))
K_VAR = (4, 18)
K_SCALE = (5, 18)
K_LOW = (6, 19)
K_TURN = ((7, 8), (19, 19))
K_PROD = (8, 8, 8, 10, 9, 10, 12, 12)
K_SCAN = (11, 14)
K_OUT = (16, 16, 16, 16)
K_RESIDUAL = 16
K_GATE = (20, 20)
K_LOGITS = 21
K_CHOOSE = ((22, 22), (22, 22), (21, 22))
K_COUNT = (23, 23, 23)
K_PLACE = ((23, 23), (24, 25), (22, 23))
K_OWNER = (25, 25, 24)
RING = 3
LEAD = 1
UB = STEPS * BH
MIX_BEATS = UNITS * UB
BEATS = MIX_BEATS + K_OWNER[PARTS - 1] + 1
PROJ_BEAT = 3
HELPED = 2
W12_HIGH_BEATS = (36, 40, 68, 70)
W12_LOW_BEATS = (65, 67, 72, 73)
SLOT_BUFS = 4
FFN_BEAT = 76
FFN_RATE = 2
WARM = 50
WARM2 = 60


def expert_pieces_at(m):
    return [divmod(i, PIECES) for i in range(max(0, (m - FFN_BEAT) * FFN_RATE), max(0, (m - FFN_BEAT + 1) * FFN_RATE))]


PIECES = 4
EARLY_PIECES = sum(len(expert_pieces_at(m)) for m in range(BEATS))
BY_SIGMOID = max(0, EARLY_PIECES // PIECES - 1)


def build_layer(nc, xT, dgT, wproj, vecs, rows, wvo, wy, w12, w3, out):
    with ExitStack() as ctx:
        def sb(name, shape, dt=F32):
            return ctx.enter_context(nc.sbuf_tensor(name, shape, dt))

        def sem(name):
            return ctx.enter_context(nc.semaphore(name))

        slots_dram = [nc.dram_tensor(f"slots{r}", [BLOCKS[r] * P, 2 * D], F32).ap() for r in range(PARTS)]
        results_dram = [nc.dram_tensor(f"results{r}", [BLOCKS[r] * P, D], F32).ap() for r in range(PARTS)]

        x_raw = sb("x_raw", [P, NB * T])
        x_parts = sb("x_parts", [P, BH * T], F32R)
        qk = sb("qk", [P, HALVES, 3, BH * T], F32R)
        dg = sb("dg", [P, 2, JT, CW])
        v = sb("v", [P, HALVES, BH, JT, D])
        mixed = sb("mixed", [P, 2, BH, CW])
        ret = sb("ret", [P, CW])
        h = sb("h", [P, HALVES, HT, D])
        centered = sb("centered", [P, 2, UT, D])
        squares = sb("squares", [P, 2, UT, D])
        normed = squares
        prelu_neg = squares[:, 0]
        stats = sb("stats", [P, 2, 5, UT])
        ssm_rows = sb("ssm_rows", [P, UT, 2 * D])
        ffn_rows = sb("ffn_rows", [P, HALVES, HT, 2 * D])
        ssm_in = sb("ssm_in", [P, BH, CW], F32R)
        gate_in = sb("gate_in", [P, BH, CW], F32R)
        keep = sb("keep", [P, 2, CW])
        take = sb("take", [P, 2, CW])
        xb = sb("xb", [P, 2, CW])
        cb = sb("cb", [P, 2, CW])
        drive = take
        state = sb("state", [P, BH, 2, CW])
        read = cb
        w_raw = mixed[:, :, :, :].rearrange("p a b n -> p (a b n)")[:, 0:WCOLS]
        w_hi = sb("w_hi", [P, WCOLS], F32R)
        w_lo = sb("w_lo", [P, WCOLS], F32R)
        gate_w = sb("gate_w", [P, 2 * NE], F32R)
        vec = sb("vec", [P, NVEC])
        neg_bd = sb("neg_bd", [P, 1])
        eps = sb("eps", [P, 1])
        spare = sb("spare", [P, 3 * UNITS])
        row = sb("row", [P, NROW])
        wy_sb = sb("wy_sb", [P, D])
        ident = sb("ident", [P, P])
        before = sb("before", [P, P], BF16)
        ones = sb("ones", [P, P], BF16)
        rank_of = sb("rank_of", [P, NE])
        ones16 = sb("ones16", [P, NE])
        block_no = sb("block_no", [1, BLOCKS[0]])
        iota_i = sb("iota_i", [P, BLOCKS[0]], I32)
        zeros = sb("zeros", [P, 256])
        logits = sb("logits", [P, HT, NE])
        best = sb("best", [P, HALVES, 2, HT])
        top = sb("top", [P, 2, HT, NE])
        scratch = [x_raw[:, k * HT * NE:(k + 1) * HT * NE] for k in range(5)]

        def token_first(k, n):
            return scratch[k][:, 0:n * NE].rearrange("p (i e) -> p i e", e=NE)

        def expert_first(k, n):
            return scratch[k][:, 0:n * NE].rearrange("p (e i) -> p e i", i=n)

        owner = x_raw[0:1, 5 * HT * NE:5 * HT * NE + BLOCKS[0] * NE].rearrange("p (n e) -> p n e", e=NE)
        r_b = sb("r_b", [P, HT])
        chosen = sb("chosen", [P, HT, NE], BF16)
        n_int = sb("n_int", [P, NE], I32)
        n_blocks = sb("n_blocks", [P, NE])
        blocks_to = sb("blocks_to", [P, NE])
        first_slot = sb("first_slot", [P, NE])
        slot_f = sb("slot_f", [P, HT, 2])
        slot_i = sb("slot_i", [P, HALVES, HT, 2], I32)
        owner_f = sb("owner_f", [1, BLOCKS[0]])
        owner_i = sb("owner_i", [1, sum(BLOCKS)], I32)
        diff = sb("diff", [P, HALVES, HT])
        expd = sb("expd", [P, HALVES, HT])
        den = sb("den", [P, HALVES, HT])
        weight = sb("weight", [P, HALVES, HT, 2])
        place = dg[:, :, :, :].rearrange("p a j t -> p (a j t)")
        wide, narrow = 2 * GB * P, 2 * GB * D

        def over_dg(at, size, c):
            return place[:, at:at + size].rearrange("p (s n c) -> p s n c", s=2, c=c)

        silu = over_dg(0, wide, HID)
        act = over_dg(wide, wide, HID)
        act_t = over_dg(2 * wide, wide, P)
        slots = place[:, 3 * wide:5 * wide].rearrange("p (s n c) -> p s n c", s=SLOT_BUFS, c=2 * D)
        res = over_dg(5 * wide, narrow, D)
        w3_sb = place[:, 5 * wide + narrow:5 * wide + narrow + NE * D]
        slots_t = qk[:, 0, 2, 0:wide].rearrange("p (s n c) -> p s n c", s=2, c=P)
        w12_hi = qk[:, 0, 0:2, :].rearrange("p a n -> p (a n)")
        w12_lo = qk[:, 1, 0:2, :].rearrange("p a n -> p (a n)")
        w12_stage = x_raw[:, BH * T:NB * T].rearrange("p (s n) -> p s n", s=2)
        back_v = x_raw[:, :].rearrange("p (h i k d) -> p h i k d", h=HALVES, k=2, d=D)

        wvo_sb = mixed[0:D, 1, 1, 0:VCOLS]
        bb = ssm_rows[:, :, :].rearrange("p i c -> p (i c)").rearrange("p (s n) -> p s n", s=2)

        ring = ctx.enter_context(nc.psum_tensor("ring", [P, 4, CW], F32))
        acc = ctx.enter_context(nc.psum_tensor("acc", [P, CW], F32))
        bank5 = ctx.enter_context(nc.psum_tensor("bank5", [P, CW], F32))
        bank6 = ctx.enter_context(nc.psum_tensor("bank6", [P, CW], F32))
        bank7 = ctx.enter_context(nc.psum_tensor("bank7", [P, CW], F32))

        ld_w, ld_vec, ld_wo, ld_wy, ld_w3 = (sem(f"ld_{n}") for n in ("w", "vec", "wo", "wy", "w3"))
        ld_w12 = [sem(f"ld_w12_{i}") for i in range(4)]
        ld_x = [sem(f"ld_x{i}") for i in range(NB)]
        ld_dg = [sem(f"ld_dg{i}") for i in range(8)]
        zeroed = sem("zeroed")
        consts_pool = sem("consts_pool")
        consts = sem("consts")
        w_split_hi, w_split = sem("w_split_hi"), sem("w_split")
        x_high, x_split = sem("x_high"), sem("x_split")
        proj_done, proj_high, proj_free = sem("proj_done"), sem("proj_high"), sem("proj_free")
        scores_done, mixed_done, pv_done, ret_done = sem("scores_done"), sem("mixed_done"), sem("pv_done"), sem("ret_done")
        gate_w_done = sem("gate_w_done")
        vo_done, bb_done = sem("vo_done"), sem("bb_done")
        y_done, y_read = sem("y_done"), sem("y_read")
        neg_done = sem("neg_done")
        mean_done = [sem("mean1"), sem("mean2")]
        center = [sem("center1"), sem("center2")]
        squared = [sem("squared1"), sem("squared2")]
        var_done = [sem("var1"), sem("var2")]
        std_done = [sem("std1"), sem("std2")]
        norm_done = [sem("norm1"), sem("norm2")]
        high_done = [sem("high1"), sem("high2")]
        rows_done = [sem("rows1"), sem("rows2")]
        turned = [sem("turned1"), sem("turned2")]
        in_done = [sem("in1"), sem("in2")]
        d_done, b_done, x_done, c_done = sem("d_done"), sem("b_done"), sem("x_done"), sem("c_done")
        sig_done, bx_done = sem("sig_done"), sem("bx_done")
        xb_done, cb_done = sem("xb_done"), sem("cb_done")
        u_done, scan_done, read_done = sem("u_done"), sem("scan_done"), sem("read_done")
        by_done, wy_done, h2_done = sem("by_done"), sem("wy_done"), sem("h2_done")
        gate_done, logits_done = sem("gate_done"), sem("logits_done")
        chosen_done, count_done, count_read = sem("chosen_done"), sem("count_done"), sem("count_read")
        slot_done, owner_done, diff_done, exp_done = sem("slot_done"), sem("owner_done"), sem("diff_done"), sem("exp_done")
        w12_hi_done, w12_lo_done = sem("w12_hi_done"), sem("w12_lo_done")
        scattered = [sem(f"scattered{i}") for i in range(PARTS)]
        ld_slots = [sem(f"ld_slots{i}") for i in range(SLOT_BUFS)]
        sturned, sin_done = sem("sturned"), sem("sin_done")
        hid_done, silu_done, act_done = sem("hid_done"), sem("silu_done"), sem("act_done")
        aturned, ain_done = sem("aturned"), sem("ain_done")
        res_done, res_read = sem("res_done"), sem("res_read")
        stored = [sem("stored0"), sem("stored1")]
        gathered = [sem(f"gathered{i}") for i in range(COMBINE0[PARTS])]
        combined = sem("combined")
        out_done = sem("out_done")
        dve_step = sem("dve_step")

        block = ctx.enter_context(nc.Block())

        def unit_of(u):
            return u // 2, u % 2

        def part_of_group(n):
            r = max(r for r in range(PARTS) if GROUP0[r] <= n)
            return r, n - GROUP0[r]

        def tiles_of(r):
            hh, c = unit_of(PART_UNITS[r][0])
            return hh, slice(c * UT, c * UT + TILES[r])

        def load_of_dg(th, j):
            return ld_dg[4 * th + j // 2]

        proj_banks = [[bank5[:, :], bank6[:, :], bank7[:, :]] + [ring[:, i, :] for i in (3, 0, 1, 2)],
                      [bank5[:, :], bank6[:, :], bank7[:, :]]]

        def proj_bank(hh, use):
            return proj_banks[hh][use % len(proj_banks[hh])]

        def side_bank(u):
            return ring[:, 3, :] if u < UNITS - 1 else bank5[:, :]

        def ssm_bank(n):
            return (bank5, bank6, bank7)[n % 3][:, :]

        def unit_h(u):
            hh, c = unit_of(u)
            return h[:, hh, c * UT:(c + 1) * UT, :]

        def rows_of(which, u):
            hh, c = unit_of(u)
            return ssm_rows[:, :, :] if which == 0 else ffn_rows[:, hh, c * UT:(c + 1) * UT, :]

        def row_of(c0, n, shape):
            return row[:, c0:c0 + n].unsqueeze(1).broadcast_to(shape)

        def add_by(eng, u):
            eng.wait_ge(center[0], u + 1)
            if u >= 1:
                eng.wait_ge(by_done, u)
            eng.tensor_tensor(unit_h(u), unit_h(u), row_of(RY, D, [P, UT, D]), ALU.add).then_inc(by_done, 1)

        def norm_low(eng, which, u):
            eng.wait_ge(high_done[which], u + 1)
            if u >= 1:
                eng.wait_ge(rows_done[which], u)
            eng.tensor_tensor(rows_of(which, u)[:, :, D:2 * D], normed[:, which], rows_of(which, u)[:, :, 0:D],
                              ALU.subtract).then_inc(rows_done[which], 1)

        def ssm_bx(eng, u, b):
            w = 2 * u + b
            eng.wait_ge(bb_done, w + 1)
            eng.wait_ge(xb_done, w + 1)
            if w >= 1:
                eng.wait_ge(bx_done, w)
            eng.tensor_tensor(xb[:, w % 2, :], bb[:, b, :], xb[:, w % 2, :], ALU.mult).then_inc(bx_done, 1)

        def ssm_read(eng, u, b):
            w = 2 * u + b
            eng.wait_ge(scan_done, w + 1)
            eng.wait_ge(cb_done, w + 1)
            if w >= 1:
                eng.wait_ge(read_done, w)
            eng.tensor_tensor(read[:, b, :], state[:, b, u % 2, :], cb[:, w % 2, :], ALU.mult).then_inc(read_done, 1)

        @block.sync
        def _(sp):
            sp.dma_start(w_raw[:, 0:V0], wproj).then_inc(ld_w, 16)
            sp.dma_start(wvo_sb, wvo).then_inc(ld_wo, 16)

            def load_x(b):
                for r in (0, D):
                    sp.dma_start(x_raw[r:r + D, b * T:(b + 1) * T], xT[b]).then_inc(ld_x[b], 16)

            load_x(0)
            sp.dma_start(vec[:, :], vecs).then_inc(ld_vec, 16)
            sp.dma_start(row[:, 0:RV], rows).then_inc(ld_vec, 16)
            load_x(1)
            for th in range(2):
                for jj in range(4):
                    sp.dma_start(dg[:, th, 2 * jj:2 * jj + 2, :],
                                 dgT[2 * jj * P:(2 * jj + 2) * P, th * CW:(th + 1) * CW]
                                 .rearrange("(a p) t -> p a t", p=P)).then_inc(ld_dg[4 * th + jj], 16)
                if th == 0:
                    sp.dma_start(wy_sb[:, :], wy).then_inc(ld_wy, 16)
                    load_x(2)
                    load_x(3)
            sp.wait_ge(consts, 1)
            for r in range(PARTS):
                flat = slots_dram[r].rearrange("(p a z c) e -> p a z (c e)", p=P, a=ZEROINGS, c=2)
                for i in range(ZEROINGS):
                    sp.dma_start(flat[:, i], zeros[:, :].unsqueeze(1).broadcast_to([P, flat.shape[2], 256])).then_inc(zeroed, 16)
            sp.wait_ge(x_split, NB)
            for i in range(4):
                if i >= 2:
                    sp.wait_ge(w12_lo_done, i - 1)
                for r in (0, D):
                    sp.dma_start(w12_stage[r:r + D, i % 2, :], w12[:, i * 1024:(i + 1) * 1024]).then_inc(ld_w12[i], 16)

            sp.wait_ge(mixed_done, MIX_BEATS)
            sp.dma_start(w3_sb[:, :], w3).then_inc(ld_w3, 16)

            def load_slots(n):
                r, g = part_of_group(n)
                if g == 0:
                    sp.wait_ge(scattered[r], 16 * 2 * TILES[r])
                if n >= SLOT_BUFS:
                    sp.wait_ge(sturned, n - SLOT_BUFS + 1)
                sp.dma_start(slots[:, n % SLOT_BUFS, :, :],
                             slots_dram[r][g * GB * P:(g + 1) * GB * P, :]
                             .rearrange("(n p) c -> p n c", p=P)).then_inc(ld_slots[n % SLOT_BUFS], 16)

            for n in range(ALL_GROUPS):
                load_slots(n)

            for r in range(PARTS):
                hh, tiles = tiles_of(r)
                for m in range(COMBINES[r]):
                    sp.wait_ge(combined, COMBINE0[r] + m + 1)
                    t0 = (tiles.start + m * LAST_TILES) // BH
                    nt = LAST_TILES // BH
                    for b in range(BH):
                        sp.dma_start(
                            out[hh * BH + b, t0 * P:(t0 + nt) * P, :].rearrange("(t p) d -> p t d", p=P),
                            h[:, hh, :, :].rearrange("p (t b) d -> p t b d", b=BH)[:, t0:t0 + nt, b, :]
                        ).then_inc(out_done, 16)
            sp.wait_ge(out_done, 16 * COMBINE0[PARTS] * BH)

        @block.gpsimd
        def _(pool):
            n = [0]

            def link(ins):
                n[0] += 1
                ins.then_inc(consts_pool, 1)
                pool.wait_ge(consts_pool, n[0])

            link(pool.memset(ones[:, :], 1.0))
            link(pool.memset(zeros[:, :], 0.0))
            link(pool.memset(ident[:, :], 0.0))
            link(pool.affine_select(out=ident[:, :], in_=ident[:, :], compare_op=ALU.not_equal, fill=1.0,
                                    base=0, pattern=[[-1, P]], channel_multiplier=1))
            link(pool.affine_select(out=before[:, :], in_=ones[:, :], compare_op=ALU.is_gt, fill=0.0,
                                    base=0, pattern=[[1, P]], channel_multiplier=-1))
            link(pool.memset(eps[:, :], EPS))
            link(pool.memset(ones16[:, :], 1.0))
            link(pool.iota(iota_i[:, 0:NE], [[-1, NE]], NE, 0))
            link(pool.tensor_copy(rank_of[:, :], iota_i[:, 0:NE]))
            link(pool.iota(iota_i[:, :], [[1, BLOCKS[0]]], 0, 0))
            pool.tensor_copy(block_no[:, :], iota_i[0:1, :]).then_inc(consts, 1)

            for b in range(BH, NB):
                pool.wait_ge(x_high, b + 1)
                pool.wait_ge(x_split, b)
                c = slice(b % BH * T, (b % BH + 1) * T)
                pool.tensor_tensor(x_parts[D:P, c], x_raw[D:P, b * T:(b + 1) * T], x_parts[D:P, c],
                                   ALU.subtract).then_inc(x_split, 1)

            for m in range(BEATS):
                for u in range(HELPED):
                    k = m - (u + 1) * UB
                    if k == K_CENTER[0][1] + 1:
                        add_by(pool, u)
                    for b in range(BH):
                        if k == K_PROD[4 * b + 2]:
                            ssm_bx(pool, u, b)
                    if k == K_SCAN[0]:
                        ssm_read(pool, u, 0)
                    for which in range(2):
                        if k == K_SCALE[which]:
                            norm_low(pool, which, u)

            def scatter(r):
                hh, tiles = tiles_of(r)
                pool.wait_ge(zeroed, 16 * PARTS * ZEROINGS)
                pool.wait_ge(rows_done[1], PART_UNITS[r][-1] + 1)
                pool.wait_ge(slot_done, r + 1)
                for i in range(tiles.start, tiles.stop):
                    for k in range(2):
                        pool.indirect_dma_start(
                            out=slots_dram[r], out_offset=bass.IndirectOffsetOnAxis(ap=slot_i[:, hh, i, k:k + 1], axis=0),
                            in_=ffn_rows[:, hh, i, :], in_offset=None).then_inc(scattered[r], 16)

            def gather(r):
                hh, tiles = tiles_of(r)
                for s in range(2):
                    pool.wait_ge(stored[s], 16 * (GROUP0[r + 1] // 2))
                if r == 0:
                    pool.wait_ge(w12_lo_done, 4)
                    pool.wait_ge(owner_done, PARTS)
                for i in range(tiles.start, tiles.stop):
                    for k in range(2):
                        pool.indirect_dma_start(
                            out=back_v[:, hh, i, k, :], out_offset=None, in_=results_dram[r],
                            in_offset=bass.IndirectOffsetOnAxis(ap=slot_i[:, hh, i, k:k + 1], axis=0)
                        ).then_inc(gathered[COMBINE0[r] + (i - tiles.start) // LAST_TILES], 16)

            for r in range(PARTS):
                scatter(r)
            for r in range(PARTS):
                gather(r)

        @block.scalar
        def _(s):
            def projections(hh, uses):
                for use in uses:
                    b, kind, th = (use - 2) // 4, (use - 2) % 4 // 2, use % 2
                    s.wait_ge(proj_done, 10 * hh + use + 1)
                    dst = qk[:, hh, 1 if kind == 0 else 0, b * T + th * CW:b * T + (th + 1) * CW]
                    s.activation(dst, proj_bank(hh, use), ACT.Identity,
                                 bias=vec[:, (BK if kind == 0 else BQ):(BK if kind == 0 else BQ) + 1]).then_inc(proj_high, 1)

            def norm_squares(which, u):
                s.wait_ge(center[which], u + 1)
                if u >= 1:
                    s.wait_ge(rows_done[which], u)
                s.activation(squares[:, which], centered[:, which], ACT.Square).then_inc(squared[which], 1)

            def norm_std(which, u):
                s.wait_ge(var_done[which], u + 1)
                s.activation(stats[:, which, 3, :], stats[:, which, 2, :], ACT.Sqrt, scale=1.0 / D,
                             bias=eps[:, 0:1]).then_inc(std_done[which], 1)

            def norm_high(which, u):
                s.wait_ge(norm_done[which], u + 1)
                if which == 0 and u >= 1:
                    s.wait_ge(turned[0], 2 * u)
                    s.wait_ge(bx_done, 2 * u)
                s.activation(rows_of(which, u)[:, :, 0:D].bitcast(F32R), normed[:, which], ACT.Copy).then_inc(high_done[which], 1)

            def take_turned(which, u, b):
                dst = ssm_in if which == 0 else gate_in
                s.wait_ge(turned[which], 2 * u + b + 1)
                if u >= 1:
                    if which == 0:
                        s.wait_ge(c_done, 2 * u)
                    else:
                        s.wait_ge(gate_done, u)
                s.activation(dst[:, b, :], (bank6, bank7)[b][:, :], ACT.Copy).then_inc(in_done[which], 1)

            def take_product(u, n):
                b, kind = divmod(n, 4)
                w = 2 * u + b
                bank = ssm_bank(n)
                s.wait_ge((d_done, b_done, x_done, c_done)[kind], w + 1)
                if kind == 0:
                    if w >= 2:
                        s.wait_ge(scan_done, w - 1)
                    s.activation(take[:, w % 2, :], bank, ACT.Sigmoid, bias=vec[:, BD:BD + 1]).then_inc(sig_done, 1)
                    s.activation(keep[:, w % 2, :], bank, ACT.Sigmoid, scale=-1.0, bias=neg_bd[:, 0:1]).then_inc(sig_done, 1)
                elif kind == 1:
                    s.wait_ge(turned[0], 2 * u + 2)
                    s.activation(bb[:, b, :], bank, ACT.Identity, bias=vec[:, BB:BB + 1]).then_inc(bb_done, 1)
                elif kind == 2:
                    if w >= 2:
                        s.wait_ge(u_done, w - 1)
                    s.activation(xb[:, w % 2, :], bank, ACT.Identity, bias=vec[:, BX:BX + 1]).then_inc(xb_done, 1)
                else:
                    if u >= 1:
                        s.wait_ge(wy_done, u)
                    s.activation(cb[:, w % 2, :], bank, ACT.Identity, bias=vec[:, BC:BC + 1]).then_inc(cb_done, 1)

            s.wait_ge(ld_w, 16)
            s.activation(w_hi[:, 0:V0], w_raw[:, 0:V0], ACT.Copy).then_inc(w_split_hi, 1)
            s.wait_ge(w_split, 1)
            s.activation(gate_w[:, 0:NE], w_hi[:, G0:G0 + NE].bitcast(F32), ACT.Copy)
            s.activation(gate_w[:, NE:2 * NE], w_lo[:, G0:G0 + NE].bitcast(F32), ACT.Copy).then_inc(gate_w_done, 1)
            s.wait_ge(vo_done, 1)
            s.activation(w_hi[:, V0:V0 + D], acc[:, 0:D], ACT.Copy).then_inc(w_split_hi, 1)

            def x_highs(hh):
                for b in range(hh * BH, (hh + 1) * BH):
                    s.wait_ge(ld_x[b], 32)
                    if b == BH:
                        s.wait_ge(proj_done, 10)
                    c = b % BH * T
                    s.activation(x_parts[:, c:c + T], x_raw[:, b * T:(b + 1) * T], ACT.Copy).then_inc(x_high, 1)

            x_highs(0)
            s.wait_ge(ld_vec, 32)
            projections(0, range(2, 10))
            s.wait_ge(consts, 1)
            x_highs(1)

            def take_y(u):
                s.wait_ge(pv_done, (u + 1) * STEPS)
                if u >= 1:
                    s.wait_ge(y_done, u)
                s.activation(ret[:, :], acc[:, :], ACT.Identity, bias=vec[:, BO:BO + 1]).then_inc(ret_done, 1)

            def w12_high(i):
                s.wait_ge(ld_w12[i], 32)
                s.wait_ge(scores_done, 2 * UB)
                c = slice(i * 1024, (i + 1) * 1024)
                s.activation(w12_hi[:, c], w12_stage[:, i % 2, :], ACT.Copy).then_inc(w12_hi_done, 1)

            def take_slots(n):
                s.wait_ge(sturned, n + 1)
                if n >= 2:
                    s.wait_ge(hid_done, n - 1)
                s.activation(slots_t[:, n % 2].rearrange("p n c -> p (n c)"), ring[:, 0, :], ACT.Copy).then_inc(sin_done, 1)

            def silus(n):
                s.wait_ge(hid_done, n + 1)
                if n >= 2:
                    s.wait_ge(act_done, n - 1)
                h1 = ring[:, 1:3, :].rearrange("p a (n c) -> p (a n) c", c=2 * HID)[:, :, 0:HID]
                s.activation(silu[:, n % 2], h1, ACT.Sigmoid if n < BY_SIGMOID else ACT.Silu).then_inc(silu_done, 1)

            def take_act(n):
                s.wait_ge(aturned, n + 1)
                if n >= 2:
                    s.wait_ge(res_done, n - 1)
                s.activation(act_t[:, n % 2].rearrange("p n c -> p (n c)"), ring[:, 3, :], ACT.Copy).then_inc(ain_done, 1)

            def store_results(n):
                r, g = part_of_group(n)
                s.wait_ge(res_read, n + 1)
                s.dma_start(results_dram[r][g * GB * P:(g + 1) * GB * P, :]
                            .rearrange("(n p) d -> p n d", p=P), res[:, n % 2]).then_inc(stored[n % 2], 16)

            def expert_piece(n, piece):
                if piece == 0 and n < ALL_GROUPS:
                    take_slots(n)
                if piece == 1 and 1 <= n <= ALL_GROUPS:
                    silus(n - 1)
                if piece == 2 and 2 <= n <= ALL_GROUPS + 1:
                    take_act(n - 2)
                if piece == 3 and n >= 4:
                    store_results(n - 4)

            for m in range(BEATS):
                if m - PROJ_BEAT in range(2, 10):
                    projections(1, [m - PROJ_BEAT])
                for u in range(UNITS):
                    k = m - (u + 1) * UB
                    if k == K_TAKE_Y:
                        take_y(u)
                    if k == K_SCALE[0] + 1:
                        s.activation(spare[:, 3 * u:3 * u + 1], eps[:, :], ACT.Sigmoid)
                    for which in range(2):
                        if k == K_CENTER[which][1] - 1:
                            s.activation(spare[:, 3 * u + 1 + which:3 * u + 2 + which], eps[:, :], ACT.Sqrt)
                        if k == K_CENTER[which][1]:
                            norm_squares(which, u)
                        if k == K_VAR[which]:
                            norm_std(which, u)
                        if k == K_SCALE[which]:
                            norm_high(which, u)
                        for b in range(BH):
                            if k == K_TURN[which][b]:
                                take_turned(which, u, b)
                    for n in range(4 * BH):
                        if k == K_PROD[n]:
                            take_product(u, n)
                if m in W12_HIGH_BEATS:
                    w12_high(W12_HIGH_BEATS.index(m))
                for n, piece in expert_pieces_at(m):
                    expert_piece(n, piece)

            for at in range(EARLY_PIECES, (ALL_GROUPS + 4) * PIECES):
                expert_piece(*divmod(at, PIECES))
            for r in range(PARTS):
                hh, tiles = tiles_of(r)
                s.wait_ge(diff_done, r + 1)
                s.activation(expd[:, hh, tiles], diff[:, hh, tiles], ACT.Exp).then_inc(exp_done, 1)

        @block.tensor
        def _(pe):
            def split_product(dst, moving, lo_col, n, last=True):
                pe.matmul(dst, w_hi[:, lo_col:lo_col + n], moving, start=True, stop=False)
                return pe.matmul(dst, w_lo[:, lo_col:lo_col + n], moving, start=False, stop=True)

            def projections(hh, uses):
                for use in uses:
                    banks = len(proj_banks[hh])
                    if use >= banks:
                        pe.wait_ge(proj_free, 10 * hh + use - banks + 1)
                    elif hh == 1:
                        pe.wait_ge(proj_free, 10)
                    if use < 2:
                        b = use
                        pe.wait_ge(x_split, hh * BH + b + 1)
                        for j in range(JT):
                            x0 = b * T + j * P
                            for part, w in enumerate((w_hi, w_lo)):
                                mm = pe.matmul(proj_bank(hh, use)[:, j * D:(j + 1) * D], x_parts[:, x0:x0 + P],
                                               w[:, V0:V0 + D], start=part == 0, stop=part == 1)
                    else:
                        b, kind, th = (use - 2) // 4, (use - 2) % 4 // 2, use % 2
                        x0 = b * T + th * CW
                        mm = split_product(proj_bank(hh, use), x_parts[:, x0:x0 + CW], K0 if kind == 0 else Q0, P)
                    mm.then_inc(proj_done, 1)

            def scores(m):
                u, j, b = m // UB, m % UB // BH, m % BH
                hh, th = unit_of(u)
                if m < BH:
                    pe.wait_ge(proj_free, 5 + 4 * b)
                elif m % UB == 0:
                    pe.wait_ge(proj_free, 10 * hh + 10)
                if m >= RING:
                    pe.wait_ge(mixed_done, m - RING + 1)
                for part in range(2):
                    mm = pe.matmul(ring[:, m % RING, :], qk[:, hh, 1 + part, b * T + j * P:b * T + (j + 1) * P],
                                   qk[:, hh, 0, b * T + th * CW:b * T + (th + 1) * CW],
                                   start=part == 0, stop=part == 1)
                mm.then_inc(scores_done, 1)

            def pv(step):
                u, j = step // STEPS, step % STEPS
                pe.wait_ge(mixed_done, BH * (step + 1))
                if j == 0 and u >= 1:
                    pe.wait_ge(ret_done, u)
                for b in range(BH):
                    mm = pe.matmul(acc[b * D:(b + 1) * D, :], v[:, u // 2, b, j, :], mixed[:, step % 2, b, :],
                                   start=j == 0, stop=j == JT - 1)
                mm.then_inc(pv_done, 1)

            def turn_y(u):
                pe.wait_ge(ret_done, u + 1)
                if u == 0:
                    pe.wait_ge(proj_free, 20)
                else:
                    pe.wait_ge(h2_done, u)
                for t in range(UT // BH):
                    mm = pe.transpose(bank5[:, t * P:(t + 1) * P], ret[:, t * P:(t + 1) * P], ident[:, :])
                mm.then_inc(y_done, 1)

            def turn_rows(which, u, b):
                rows_ = rows_of(which, u)
                pe.wait_ge(rows_done[which], u + 1)
                if which == 1:
                    pe.wait_ge(bb_done, 2 * u + 2)
                    pe.wait_ge(cb_done, 2 * u + 2)
                elif u == 0:
                    pe.wait_ge(proj_free, 20)
                else:
                    pe.wait_ge(in_done[1], 2 * u)
                for t in range(UT // BH):
                    mm = pe.transpose((bank6, bank7)[b][:, t * P:(t + 1) * P], rows_[:, t * BH + b, :], ident[:, :])
                mm.then_inc(turned[which], 1)

            def product(u, n):
                b, kind = divmod(n, 4)
                w = 2 * u
                pe.wait_ge(in_done[0], w + b + 1)
                before_ = ((y_read, u + 1), (in_done[0], w + 1), (in_done[0], w + 2), (sig_done, 2 * w + 2),
                           (bb_done, w + 1), (xb_done, w + 1), (cb_done, w + 1), (sig_done, 2 * w + 4))[n]
                pe.wait_ge(*before_)
                split_product(ssm_bank(n), ssm_in[:, b, :], (D0, B0, X0, C0)[kind], CH
                              ).then_inc((d_done, b_done, x_done, c_done)[kind], 1)

            def ssm_out(u, part):
                if u == 0:
                    pe.wait_ge(ld_wy, 16)
                pe.wait_ge(xb_done, 2 * u + 2)
                pe.wait_ge(read_done, 2 * u + 2)
                n = UT // len(K_OUT)
                for i in range(part * n, (part + 1) * n):
                    b, t = i % BH, i // BH
                    mm = pe.matmul(bank5[:, i * D:(i + 1) * D], read[:, b, t * P:(t + 1) * P], wy_sb[:, :],
                                   start=True, stop=True)
                if part == len(K_OUT) - 1:
                    mm.then_inc(wy_done, 1)

            def gate(u, part):
                pe.wait_ge(gate_w_done, 1)
                pe.wait_ge(in_done[1], 2 * u + 2)
                pe.wait_ge(proj_free, 10)
                if u == UNITS - 1:
                    pe.wait_ge(h2_done, UNITS)
                elif u >= 1:
                    pe.wait_ge(logits_done, u)
                    if u >= 2:
                        pe.wait_ge(count_read, u - 1)
                n = UT // len(K_GATE)
                for i in range(part * n, (part + 1) * n):
                    b, t = i % BH, i // BH
                    mm = pe.matmul(side_bank(u)[:, i * 2 * NE:(i + 1) * 2 * NE], gate_in[:, b, t * P:(t + 1) * P],
                                   gate_w[:, :], start=True, stop=True)
                if part == len(K_GATE) - 1:
                    mm.then_inc(gate_done, 1)

            def count(r):
                _, tiles = tiles_of(r)
                n = TILES[r] * NE
                side = side_bank(PART_UNITS[r][-1])
                pe.wait_ge(chosen_done, r + 1)
                picked = chosen[:, tiles, :].rearrange("p i e -> p (i e)")
                pe.matmul(side[:, 0:n], before[:, :], picked, start=True, stop=True)
                pe.matmul(side[:, n:2 * n], ones[:, :], picked, start=True, stop=True).then_inc(count_done, 1)

            pe.wait_ge(consts_pool, 1)
            def warm_up(n):
                for i in range(n):
                    pe.matmul(ring[:, 0, 0:P], ones[:, :], ones[:, :], start=True, stop=True)

            warm_up(WARM)
            pe.wait_ge(ld_wo, 16)
            pe.matmul(acc[:, 0:D], wvo_sb[:, VW:VW + P], wvo_sb[:, VO:VO + D], start=True, stop=True)
            pe.matmul(acc[:, D:2 * D], wvo_sb[:, VB:VB + P], wvo_sb[:, VO:VO + D], start=True, stop=True).then_inc(vo_done, 1)
            warm_up(WARM2)
            pe.wait_ge(w_split, 2)
            projections(0, range(10))
            pe.wait_ge(consts, 1)
            experts = {}

            def turn_slots(n):
                pe.wait_ge(ld_slots[n % SLOT_BUFS], 16 * (n // SLOT_BUFS + 1))
                if n >= 1:
                    pe.wait_ge(sin_done, n)
                for k in range(GB):
                    mm = pe.transpose(ring[:, 0, k * P:(k + 1) * P], slots[:, n % SLOT_BUFS, k, :], ident[:, :])
                mm.then_inc(sturned, 1)

            def hidden(n):
                r, g = part_of_group(n)
                if g == 0:
                    pe.wait_ge(owner_done, r + 1)
                if n == 0:
                    pe.wait_ge(w12_lo_done, 4)
                _, experts[n] = nc.values_load_multi_w_load_instructions(
                    owner_i[0:1, n * GB:(n + 1) * GB], engines=[PE_ENGINE], min_val=0, max_val=NE - 1,
                    skip_runtime_bounds_check_because="the owner of a block is at most NE - 1")
                pe.wait_ge(sin_done, n + 1)
                if n >= 1:
                    pe.wait_ge(act_done, n)
                for k in range(GB):
                    for part, w in enumerate((w12_hi, w12_lo)):
                        mm = pe.matmul(ring[:, 1 + k // 2, k % 2 * 2 * HID:(k % 2 + 1) * 2 * HID], slots_t[:, n % 2, k, :],
                                       w[:, bass.ds(experts[n][k] * (2 * HID), 2 * HID)], start=part == 0, stop=part == 1)
                mm.then_inc(hid_done, 1)

            def turn_act(n):
                pe.wait_ge(act_done, n + 1)
                if n >= 1:
                    pe.wait_ge(ain_done, n)
                else:
                    pe.wait_ge(count_read, PARTS - 1)
                for k in range(GB):
                    mm = pe.transpose(ring[:, 3, k * P:(k + 1) * P], act[:, n % 2, k, :], ident[:, :])
                mm.then_inc(aturned, 1)

            def result(n):
                if n == 0:
                    pe.wait_ge(ld_w3, 16)
                    pe.wait_ge(ret_done, UNITS)
                else:
                    pe.wait_ge(res_read, n)
                pe.wait_ge(ain_done, n + 1)
                for k in range(GB):
                    mm = pe.matmul(acc[:, k * D:(k + 1) * D], act_t[:, n % 2, k, :],
                                   w3_sb[:, bass.ds(experts[n][k] * D, D)], start=True, stop=True)
                mm.then_inc(res_done, 1)

            def expert_piece(n, piece):
                if n == 0 and piece == 0:
                    pe.wait_ge(mixed_done, MIX_BEATS)
                if piece == 0 and n < ALL_GROUPS:
                    turn_slots(n)
                if piece == 1 and 1 <= n <= ALL_GROUPS:
                    hidden(n - 1)
                if piece == 2 and 2 <= n <= ALL_GROUPS + 1:
                    turn_act(n - 2)
                if piece == 3 and n >= 3:
                    result(n - 3)

            for m in range(LEAD):
                scores(m)
            for m in range(BEATS):
                if m + LEAD < MIX_BEATS:
                    scores(m + LEAD)
                if m % BH == 1 and BH < m <= MIX_BEATS + 1:
                    pv(m // BH - 1)
                if m - PROJ_BEAT in range(10):
                    projections(1, [m - PROJ_BEAT])
                for u in range(UNITS):
                    k = m - (u + 1) * UB
                    if k == K_TURN_Y:
                        turn_y(u)
                    for b in range(BH):
                        if k == K_TURN[0][b]:
                            turn_rows(0, u, b)
                    for n in range(4 * BH):
                        if k == K_PROD[n]:
                            product(u, n)
                    for part, at in enumerate(K_OUT):
                        if k == at:
                            ssm_out(u, part)
                    for b in range(BH):
                        if k == K_TURN[1][b]:
                            turn_rows(1, u, b)
                    for part, at in enumerate(K_GATE):
                        if k == at:
                            gate(u, part)
                    if u in PART_OF and k == K_COUNT[PART_OF[u]]:
                        count(PART_OF[u])
                for n, piece in expert_pieces_at(m):
                    expert_piece(n, piece)

            for at in range(EARLY_PIECES, (ALL_GROUPS + 3) * PIECES):
                expert_piece(*divmod(at, PIECES))

        @block.vector
        def _(dve):
            steps = [0]

            def link(ins):
                steps[0] += 1
                ins.then_inc(dve_step, 1)
                dve.wait_ge(dve_step, steps[0])

            def x_lows():
                for b in range(BH):
                    dve.wait_ge(x_high, b + 1)
                    c = slice(b % BH * T, (b % BH + 1) * T)
                    dve.tensor_tensor(x_parts[D:P, c], x_raw[D:P, b * T:(b + 1) * T], x_parts[D:P, c],
                                      ALU.subtract).then_inc(x_split, 1)

            def projections(hh, uses):
                for use in uses:
                    if use < 2:
                        dve.wait_ge(proj_done, 10 * hh + use + 1)
                        dve.tensor_tensor(v[:, hh, use], proj_bank(hh, use).rearrange("p (j d) -> p j d", d=D),
                                          row_of(RV, D, [P, JT, D]), ALU.add).then_inc(proj_free, 1)
                        continue
                    b, kind, th = (use - 2) // 4, (use - 2) % 4 // 2, use % 2
                    c = slice(b * T + th * CW, b * T + (th + 1) * CW)
                    dve.wait_ge(proj_high, 8 * hh + use - 1)
                    r = slice(0, P) if kind == 0 else slice(D, P)
                    dve.scalar_tensor_tensor(out=qk[r, hh, 2 if kind == 0 else 0, c], in0=proj_bank(hh, use)[r, :],
                                             scalar=vec[r, (BK if kind == 0 else BQ):(BK if kind == 0 else BQ) + 1],
                                             in1=qk[r, hh, 1 if kind == 0 else 0, c], op0=ALU.add, op1=ALU.subtract
                                             ).then_inc(proj_free, 1)

            def mix_beat(m):
                u, j, b = m // UB, m % UB // BH, m % BH
                if u < 2 and j % 2 == 0 and b == 0:
                    dve.wait_ge(load_of_dg(u, j), 16)
                dve.wait_ge(scores_done, m + 1)
                if m >= 2 * BH:
                    dve.wait_ge(pv_done, m // BH - 1)
                dve.tensor_tensor(mixed[:, m // BH % 2, b, :], ring[:, m % RING, :], dg[:, u % 2, j, :],
                                  ALU.mult).then_inc(mixed_done, 1)

            def prelu(u, part):
                y = bank5[:, :].rearrange("p (i d) -> p i d", d=D)
                if part == 0:
                    dve.wait_ge(y_done, u + 1)
                    if u >= 1:
                        dve.wait_ge(rows_done[0], u)
                    dve.tensor_scalar(prelu_neg, y, 0.0, vec[:, PRELU:PRELU + 1], ALU.min, ALU.mult).then_inc(neg_done, 1)
                else:
                    dve.wait_ge(neg_done, u + 1)
                    dve.scalar_tensor_tensor(out=unit_h(u), in0=y, scalar=0.0, in1=prelu_neg, op0=ALU.max,
                                             op1=ALU.add).then_inc(y_read, 1)

            def norm_mean(which, u):
                dve.wait_ge((y_read, h2_done)[which], u + 1)
                link(dve.tensor_reduce(stats[:, which, 0, :], unit_h(u), AX_X, ALU.add))
                dve.tensor_scalar(stats[:, which, 1, :], stats[:, which, 0, :], -1.0 / D, None, ALU.mult
                                  ).then_inc(mean_done[which], 1)

            def norm_center(which, u):
                dve.wait_ge(mean_done[which], u + 1)
                dve.tensor_tensor(centered[:, which], unit_h(u), stats[:, which, 1, :].unsqueeze(2).broadcast_to([P, UT, D]),
                                  ALU.add).then_inc(center[which], 1)

            def norm_var(which, u):
                dve.wait_ge(squared[which], u + 1)
                dve.tensor_reduce(stats[:, which, 2, :], squares[:, which], AX_X, ALU.add).then_inc(var_done[which], 1)

            def norm_scale(which, u):
                dve.wait_ge(std_done[which], u + 1)
                link(dve.reciprocal(stats[:, which, 4, :], stats[:, which, 3, :]))
                if u >= 1:
                    dve.wait_ge(high_done[which], u)
                dve.tensor_tensor(normed[:, which], centered[:, which],
                                  stats[:, which, 4, :].unsqueeze(2).broadcast_to([P, UT, D]), ALU.mult).then_inc(norm_done[which], 1)

            def ssm_scan(u, b):
                w = 2 * u + b
                dve.wait_ge(bx_done, w + 1)
                dve.wait_ge(sig_done, 2 * w + 2)
                dve.tensor_tensor(drive[:, w % 2, :], take[:, w % 2, :], xb[:, w % 2, :], ALU.mult).then_inc(u_done, 1)
                dve.wait_ge(u_done, w + 1)
                if u >= 2:
                    dve.wait_ge(read_done, w - 3)
                start = 0.0 if u % 2 == 0 else state[:, b, 0, CW - 1:CW]
                dve.tensor_tensor_scan(state[:, b, u % 2, :], keep[:, w % 2, :], drive[:, w % 2, :], start,
                                       ALU.mult, ALU.add).then_inc(scan_done, 1)

            def residual(u):
                hu = unit_h(u)
                dve.wait_ge(wy_done, u + 1)
                dve.wait_ge(by_done, u + 1)
                dve.tensor_tensor(hu, bank5[:, :].rearrange("p (i d) -> p i d", d=D), hu, ALU.add).then_inc(h2_done, 1)

            def w12_low(i):
                dve.wait_ge(scores_done, MIX_BEATS)
                dve.wait_ge(w12_hi_done, i + 1)
                c = slice(i * 1024, (i + 1) * 1024)
                dve.tensor_tensor(w12_lo[:, c], w12_stage[:, i % 2, :], w12_hi[:, c], ALU.subtract).then_inc(w12_lo_done, 1)

            def take_logits(u):
                hh, c = unit_of(u)
                dve.wait_ge(gate_done, u + 1)
                parts = side_bank(u)[:, 0:2 * UT * NE].rearrange("p (i a e) -> p i a e", a=2, e=NE)
                lg = logits[:, c * UT:(c + 1) * UT, :]
                link(dve.tensor_tensor(lg, parts[:, :, 0, :], row_of(RG, NE, [P, UT, NE]), ALU.add))
                dve.tensor_tensor(lg, parts[:, :, 1, :], lg, ALU.add).then_inc(logits_done, 1)

            def choose(r, k):
                hh, tiles = tiles_of(r)
                full = [P, TILES[r], NE]
                lg, mark, score = logits[:, tiles, :], token_first(0, TILES[r]), r_b[:, tiles]
                if k == 0:
                    dve.wait_ge(logits_done, PART_UNITS[r][-1] + 1)
                high = best[:, hh, k, tiles]
                link(dve.tensor_reduce(high, lg, AX_X, ALU.max))
                link(dve.tensor_tensor(mark, lg, high.unsqueeze(2).broadcast_to(full), ALU.is_equal))
                link(dve.tensor_tensor(mark, mark, rank_of[:, :].unsqueeze(1).broadcast_to(full), ALU.mult))
                link(dve.tensor_reduce(score, mark, AX_X, ALU.max))
                link(dve.tensor_tensor(top[:, k, tiles], mark, score.unsqueeze(2).broadcast_to(full), ALU.is_equal))
                if k == 0:
                    link(dve.scalar_tensor_tensor(out=lg, in0=top[:, 0, tiles], scalar=-3e38, in1=lg,
                                                  op0=ALU.mult, op1=ALU.add))
                    return
                dve.tensor_tensor(chosen[:, tiles, :], top[:, 0, tiles], top[:, 1, tiles], ALU.add).then_inc(chosen_done, 1)
                dve.tensor_tensor(diff[:, hh, tiles], best[:, hh, 1, tiles], best[:, hh, 0, tiles],
                                  ALU.subtract).then_inc(diff_done, 1)

            def place_experts(r):
                nt = TILES[r]
                side = side_bank(PART_UNITS[r][-1])
                counts, counts_to, not_first = (expert_first(k, nt) for k in (2, 3, 4))
                flat = "p e i -> p (e i)"
                link(dve.memset(not_first, 1.0))
                link(dve.memset(not_first[:, :, 0:1], 0.0))
                dve.wait_ge(count_done, r + 1)
                in_tile = side[:, nt * NE:2 * nt * NE].rearrange("p (i e) -> p e i", e=NE)
                link(dve.tensor_copy(counts, in_tile))
                link(dve.tensor_tensor_scan(counts_to.rearrange(flat), not_first.rearrange(flat),
                                            counts.rearrange(flat), 0.0, ALU.mult, ALU.add))
                link(dve.tensor_scalar(n_int[:, :], counts_to[:, :, nt - 1], float(P - 1), None, ALU.add))
                link(dve.tensor_scalar(n_int[:, :], n_int[:, :], 7, None, ALU.logical_shift_right))
                link(dve.tensor_copy(n_blocks[:, :], n_int[:, :]))
                link(dve.tensor_tensor_scan(blocks_to[:, :], ones16[:, :], n_blocks[:, :], 0.0, ALU.mult, ALU.add))
                link(dve.tensor_tensor(first_slot[:, :], blocks_to[:, :], n_blocks[:, :], ALU.subtract))
                link(dve.tensor_tensor(counts_to, counts_to, counts, ALU.subtract))

            def place_tokens(r):
                hh, tiles = tiles_of(r)
                nt = TILES[r]
                slot, found, offset = token_first(1, nt), token_first(0, nt), expert_first(3, nt)
                before_it = side_bank(PART_UNITS[r][-1])[:, 0:nt * NE].rearrange("p (i e) -> p i e", e=NE)
                link(dve.scalar_tensor_tensor(out=offset, in0=first_slot[:, :].unsqueeze(2).broadcast_to([P, NE, nt]),
                                              scalar=float(P), in1=offset, op0=ALU.mult, op1=ALU.add))
                dve.tensor_tensor(slot, before_it, offset.rearrange("p e i -> p i e"), ALU.add).then_inc(count_read, 1)
                dve.wait_ge(count_read, r + 1)
                for k in range(2):
                    link(dve.tensor_tensor(found, slot, top[:, k, tiles], ALU.mult))
                    link(dve.tensor_reduce(slot_f[:, tiles, k], found, AX_X, ALU.add))
                dve.tensor_copy(slot_i[:, hh, tiles], slot_f[:, tiles, :]).then_inc(slot_done, 1)

            def owners(r):
                n, at = BLOCKS[r], GROUP0[r] * GB
                link(dve.tensor_tensor(owner[:, 0:n, :], blocks_to[0:1, :].unsqueeze(1).broadcast_to([1, n, NE]),
                                       block_no[:, 0:n].unsqueeze(2).broadcast_to([1, n, NE]), ALU.is_le))
                link(dve.tensor_reduce(owner_f[:, 0:n], owner[:, 0:n, :], AX_X, ALU.add))
                link(dve.tensor_scalar(owner_f[:, 0:n], owner_f[:, 0:n], float(NE - 1), None, ALU.min))
                dve.tensor_copy(owner_i[:, at:at + n], owner_f[:, 0:n]).then_inc(owner_done, 1)

            def weights(r):
                hh, tiles = tiles_of(r)
                dve.wait_ge(exp_done, r + 1)
                link(dve.tensor_scalar(den[:, hh, tiles], expd[:, hh, tiles], 1.0, None, ALU.add))
                link(dve.reciprocal(weight[:, hh, tiles, 0], den[:, hh, tiles]))
                link(dve.tensor_tensor(weight[:, hh, tiles, 1], expd[:, hh, tiles], weight[:, hh, tiles, 0], ALU.mult))

            def gated(n):
                dve.wait_ge(silu_done, n + 1)
                both = ring[:, 1:3, :].rearrange("p a (n c) -> p (a n) c", c=2 * HID)
                if n < BY_SIGMOID:
                    link(dve.tensor_tensor(silu[:, n % 2], both[:, :, 0:HID], silu[:, n % 2], ALU.mult))
                if n >= 2:
                    dve.wait_ge(aturned, n - 1)
                dve.tensor_tensor(act[:, n % 2], both[:, :, HID:2 * HID], silu[:, n % 2], ALU.mult).then_inc(act_done, 1)

            def take_result(n):
                dve.wait_ge(res_done, n + 1)
                if n >= 2:
                    dve.wait_ge(stored[n % 2], 16 * (n // 2))
                dve.tensor_copy(res[:, n % 2], acc[:, 0:GB * D].rearrange("p (n d) -> p n d", d=D)).then_inc(res_read, 1)

            def expert_piece(n, piece):
                if piece == 2 and 1 <= n <= ALL_GROUPS:
                    gated(n - 1)
                if piece == 3 and n >= 3:
                    take_result(n - 3)

            dve.wait_ge(w_split_hi, 1)
            dve.tensor_tensor(w_lo[:, 0:V0], w_raw[:, 0:V0], w_hi[:, 0:V0], ALU.subtract).then_inc(w_split, 1)
            dve.wait_ge(w_split_hi, 2)
            dve.tensor_tensor(w_lo[:, V0:V0 + D], acc[:, 0:D], w_hi[:, V0:V0 + D], ALU.subtract).then_inc(w_split, 1)
            link(dve.tensor_copy(row[:, RV:RV + D], acc[:, D:2 * D]))
            x_lows()
            dve.wait_ge(ld_vec, 32)
            link(dve.tensor_scalar(neg_bd[:, :], vec[:, BD:BD + 1], -1.0, None, ALU.mult))
            projections(0, range(10))
            dve.wait_ge(consts, 1)
            for m in range(BEATS):
                if m < MIX_BEATS:
                    mix_beat(m)
                if m - PROJ_BEAT in range(2):
                    projections(1, [m - PROJ_BEAT])
                if m - PROJ_BEAT - 1 in range(2, 10):
                    projections(1, [m - PROJ_BEAT - 1])
                for u in range(UNITS):
                    k = m - (u + 1) * UB
                    for part in range(2):
                        if k == K_PRELU[part]:
                            prelu(u, part)
                    if k == K_RESIDUAL:
                        residual(u)
                    for which in range(2):
                        if k == K_CENTER[which][0]:
                            norm_mean(which, u)
                        if k == K_CENTER[which][1]:
                            norm_center(which, u)
                        if k == K_VAR[which]:
                            norm_var(which, u)
                        if k == K_SCALE[which]:
                            norm_scale(which, u)
                        if k == K_LOW[which] and u >= HELPED:
                            norm_low(dve, which, u)
                    if k == K_CENTER[0][1] + 1 and u >= HELPED:
                        add_by(dve, u)
                    for b in range(BH):
                        if k == K_SCAN[b]:
                            if u >= HELPED:
                                ssm_bx(dve, u, b)
                            ssm_scan(u, b)
                            if u >= HELPED or b == BH - 1:
                                ssm_read(dve, u, b)
                    if k == K_LOGITS:
                        take_logits(u)
                    for which in range(2):
                        if u in PART_OF and k == K_CHOOSE[PART_OF[u]][which]:
                            choose(PART_OF[u], which)
                    for which, place in enumerate((place_experts, place_tokens)):
                        if u in PART_OF and k == K_PLACE[PART_OF[u]][which]:
                            place(PART_OF[u])
                    if u in PART_OF and k == K_OWNER[PART_OF[u]]:
                        owners(PART_OF[u])
                if m in W12_LOW_BEATS:
                    w12_low(W12_LOW_BEATS.index(m))
                for n, piece in expert_pieces_at(m):
                    expert_piece(n, piece)

            for at in range(EARLY_PIECES, (ALL_GROUPS + 3) * PIECES):
                expert_piece(*divmod(at, PIECES))

            for r in range(PARTS):
                weights(r)
                hh, tiles = tiles_of(r)
                for m in range(COMBINES[r]):
                    i = slice(tiles.start + m * LAST_TILES, tiles.start + (m + 1) * LAST_TILES)
                    dve.wait_ge(gathered[COMBINE0[r] + m], 16 * 2 * LAST_TILES)
                    got = back_v[:, hh, i]
                    link(dve.tensor_tensor(got, got, weight[:, hh, i, :].unsqueeze(3).broadcast_to([P, LAST_TILES, 2, D]), ALU.mult))
                    link(dve.tensor_tensor(h[:, hh, i], h[:, hh, i], got[:, :, 0, :], ALU.add))
                    dve.tensor_tensor(h[:, hh, i], h[:, hh, i], got[:, :, 1, :], ALU.add).then_inc(combined, 1)


def kernel(**inputs):
    import numpy as np
    import concourse.bacc as bacc
    from concourse.bass_utils import run_bass_kernel_spmd as run

    def a(name):
        return np.asarray(inputs[name])

    def both(m):
        return np.concatenate([m, m], axis=0)

    wq, wk, wbc = a("L0_tok_Wq"), a("L0_tok_Wk"), a("L0_attn_Wbc")
    n = wbc.shape[1] // 2
    bbc = a("L0_attn_bbc")
    wproj = both(np.concatenate([wq, wq, wk, wk, a("L0_attn_Wx"), wbc[:, :n], wbc[:, n:],
                                 a("L0_attn_Wd"), a("L0_ffn_gate_w")], axis=1))
    vecs = np.stack([both(a("L0_tok_bq")), both(a("L0_tok_bk")), a("L0_attn_bx"), bbc[:n], bbc[n:], a("L0_attn_bd"),
                     np.broadcast_to(a("L0_tok_prelu_a"), (P,)), both(a("L0_tok_bo"))], axis=1)
    rows = np.broadcast_to(np.concatenate([a("L0_attn_by"), a("L0_ffn_gate_b")]), (P, RV))
    wv_t = a("L0_tok_Wv").T
    wvo = np.concatenate([wv_t, wv_t, np.broadcast_to(a("L0_tok_bv")[:, None], (D, P)), a("L0_tok_Wo")], axis=1)
    w12 = np.concatenate([a("L0_ffn_w1"), a("L0_ffn_w2")], axis=2).transpose(1, 0, 2).reshape(D, -1)
    arrays = {
        "xT": a("x").reshape(NB, T, D).transpose(0, 2, 1),
        "dgT": a("L0_tok_d_gamma_batched").T,
        "wproj": wproj, "vecs": vecs, "rows": rows,
        "wvo": wvo, "wy": a("L0_attn_Wy"), "w12": w12,
        "w3": a("L0_ffn_w3").transpose(1, 0, 2).reshape(HID, -1),
    }
    arrays = {k: np.ascontiguousarray(m) for k, m in arrays.items()}
    nc = bacc.Bacc("TRN2", target_bir_lowering=False, num_devices=1)
    args = [nc.dram_tensor(k, m.shape, mybir.dt.from_np(m.dtype), kind="ExternalInput").ap() for k, m in arrays.items()]
    out = nc.dram_tensor("out", (NB, T, D), F32, kind="ExternalOutput").ap()
    build_layer(nc, *args, out)
    r = run(nc, [arrays], core_ids=[0])
    return r.results[0]["out"]
```
